# Optimizing a Trainium2 kernel written in Bass

```python
import numpy as np
import jax
import jax.numpy as jnp

def _softmax(x, axis=-1):
    return jax.nn.softmax(x, axis=axis)

def _gelu(x):
    return jax.nn.gelu(x, approximate=True)

def _silu(x):
    return jax.nn.silu(x)

def _sigmoid(x):
    return jax.nn.sigmoid(x)

def _layernorm(x, axis=-1, eps=1e-05):
    m = jnp.mean(x, axis=axis, keepdims=True)
    v = jnp.var(x, axis=axis, keepdims=True)
    return (x - m) / jnp.sqrt(v + eps)

def _scatter_add(tgt, idx, src, axis=0):
    return tgt.at[idx].add(src)

def _segment_sum(src, seg, n):
    return jax.ops.segment_sum(src, seg, n)
kernel_name = 'mk_lm_tower_d2_tok_ids512_r4_e3dd0d'

def setup_inputs(seed: int=0):
    np.random.seed(seed)
    _w = jnp.asarray

    def _rec_inputs():
        import jax
        import jax.numpy as jnp
        _rk = jax.random.key(seed)
        x = jax.random.randint(jax.random.fold_in(_rk, 1), (16, 512), 0, 8000, jnp.int32)
        return x
    x = _rec_inputs()

    def _L0_tok_setup():
        import jax, jax.numpy as jnp
        import numpy as np
        VOCAB = 8000
        EMB = 128
        K = 3
        B, T = (8, 1024)
        key = jax.random.key(seed)
        k_ids, k_w = jax.random.split(key)
        token_ids = jax.random.randint(k_ids, (B, T), 0, VOCAB, dtype=jnp.int64)
        conv_w = jax.random.normal(k_w, (EMB, VOCAB, K), dtype=jnp.float32) * 0.02
        return {'token_ids': token_ids, 'conv_w': conv_w}
    _L0_tok_all = _L0_tok_setup()
    _L0_tok_in = {k: v for k, v in _L0_tok_all.items() if k in ('conv_w',)}
    del _L0_tok_all

    def _L0_attn_setup():
        import jax, jax.numpy as jnp
        import numpy as np
        D_MODEL, N_HEADS, D_KEYS, D_LLM = (128, 8, 16, 1024)
        B, L, S = (32, 256, 250)
        HE = N_HEADS * D_KEYS
        key = jax.random.key(seed)
        ks = jax.random.split(key, 11)
        s = 0.02
        return {'target_embedding': jax.random.normal(ks[0], (B, L, D_MODEL), jnp.float32), 'source_embedding': jax.random.normal(ks[1], (S, D_LLM), jnp.float32), 'value_embedding': jax.random.normal(ks[2], (S, D_LLM), jnp.float32), 'Wq': jax.random.normal(ks[3], (D_MODEL, HE), jnp.float32) * s, 'bq': jnp.zeros((HE,), jnp.float32), 'Wk': jax.random.normal(ks[4], (D_LLM, HE), jnp.float32) * s, 'bk': jnp.zeros((HE,), jnp.float32), 'Wv': jax.random.normal(ks[5], (D_LLM, HE), jnp.float32) * s, 'bv': jnp.zeros((HE,), jnp.float32), 'Wo': jax.random.normal(ks[6], (HE, D_MODEL), jnp.float32) * s, 'bo': jnp.zeros((D_MODEL,), jnp.float32)}
    _L0_attn_all = _L0_attn_setup()
    _L0_attn_in = {k: v for k, v in _L0_attn_all.items() if k in ('source_embedding', 'value_embedding', 'Wq', 'bq', 'Wk', 'bk', 'Wv', 'bv', 'Wo', 'bo')}
    del _L0_attn_all

    def _L0_ffn_setup():
        import jax, jax.numpy as jnp
        import numpy as np
        MARK_AX = 0
        OP_AND = 1
        OP_OR = 2
        OP_XOR = 3
        ALU_LO = 16
        ALU_HI = 32
        AX_CARRY_LO = 48
        AX_CARRY_HI = 64
        OUTPUT_LO = 80
        OUTPUT_HI = 96
        NIB_A = 0
        NIB_B = 1
        OP_START = 16
        RESULT = 64
        GE_DIM = 160
        N_ROWS = 8
        B, S, D = (8, 1024, 128)

        def _decode_nibble(x_bd, start):
            bits = x_bd[..., start:start + 16] > 0.5
            return jnp.argmax(bits, axis=-1).astype(x_bd.dtype)

        def _mlp2(x, w1, b1, w2, b2):
            h = jax.nn.relu(jnp.einsum('bsrd,de->bsre', x, w1) + b1)
            return jnp.einsum('bsrd,de->bsre', h, w2) + b2

        def _forward(x_bd, and_w1, and_b1, and_w2, and_b2, or_w1, or_b1, or_w2, or_b2, xor_w1, xor_b1, xor_w2, xor_b2):
            a_lo = _decode_nibble(x_bd, ALU_LO)
            a_hi = _decode_nibble(x_bd, ALU_HI)
            b_lo = _decode_nibble(x_bd, AX_CARRY_LO)
            b_hi = _decode_nibble(x_bd, AX_CARRY_HI)
            Bsz, Ssz, _ = x_bd.shape
            x_ge = jnp.zeros((Bsz, Ssz, N_ROWS, GE_DIM), x_bd.dtype)
            x_ge = x_ge.at[..., 0, NIB_A].set(a_lo).at[..., 1, NIB_A].set(a_hi)
            x_ge = x_ge.at[..., 0, NIB_B].set(b_lo).at[..., 1, NIB_B].set(b_hi)
            x_ge = x_ge.at[..., :, OP_START + 28].set(x_bd[..., OP_OR, None])
            x_ge = x_ge.at[..., :, OP_START + 29].set(x_bd[..., OP_XOR, None])
            x_ge = x_ge.at[..., :, OP_START + 30].set(x_bd[..., OP_AND, None])
            y_and = _mlp2(x_ge, and_w1, and_b1, and_w2, and_b2)
            y_or = _mlp2(x_ge, or_w1, or_b1, or_w2, or_b2)
            y_xor = _mlp2(x_ge, xor_w1, xor_b1, xor_w2, xor_b2)
            is_and = x_bd[..., OP_AND] > 0.5
            is_or = x_bd[..., OP_OR] > 0.5
            is_xor = x_bd[..., OP_XOR] > 0.5
            sel = jnp.where(is_and[..., None, None], y_and, jnp.where(is_or[..., None, None], y_or, y_xor))
            active = (x_bd[..., MARK_AX] >= 0.5) & (is_and | is_or | is_xor)
            res_lo = jnp.clip(jnp.round(sel[..., 0, RESULT]), 0, 15).astype(jnp.int32)
            res_hi = jnp.clip(jnp.round(sel[..., 1, RESULT]), 0, 15).astype(jnp.int32)
            amask = active.astype(x_bd.dtype)[..., None]
            add_lo = 2.0 * jax.nn.one_hot(res_lo, 16, dtype=x_bd.dtype) * amask
            add_hi = 2.0 * jax.nn.one_hot(res_hi, 16, dtype=x_bd.dtype) * amask
            out = x_bd.at[..., OUTPUT_LO:OUTPUT_LO + 16].add(add_lo)
            out = out.at[..., OUTPUT_HI:OUTPUT_HI + 16].add(add_hi)
            return out
        key = jax.random.key(seed)
        ks = jax.random.split(key, 7)
        inp = {'x_bd': jax.random.uniform(ks[0], (B, S, D), dtype=jnp.float32)}
        for i, op in enumerate(['and', 'or', 'xor']):
            inp[op + '_w1'] = jax.random.normal(ks[1 + 2 * i], (GE_DIM, GE_DIM), jnp.float32) * 0.08
            inp[op + '_b1'] = jnp.zeros((GE_DIM,), jnp.float32)
            inp[op + '_w2'] = jax.random.normal(ks[2 + 2 * i], (GE_DIM, GE_DIM), jnp.float32) * 0.08
            inp[op + '_b2'] = jnp.zeros((GE_DIM,), jnp.float32)
        return inp
    _L0_ffn_all = _L0_ffn_setup()
    _L0_ffn_in = {k: v for k, v in _L0_ffn_all.items() if k in ('and_w1', 'and_b1', 'and_w2', 'and_b2', 'or_w1', 'or_b1', 'or_w2', 'or_b2', 'xor_w1', 'xor_b1', 'xor_w2', 'xor_b2')}
    del _L0_ffn_all

    def _L1_attn_setup():
        import jax, jax.numpy as jnp
        import numpy as np
        LN_EPS = 1e-05
        RMS_EPS = 1.1920929e-07

        def _layernorm(x, g, b):
            m = jnp.mean(x, axis=-1, keepdims=True)
            xc = x - m
            v = jnp.mean(xc * xc, axis=-1, keepdims=True)
            return xc / jnp.sqrt(v + LN_EPS) * g + b
        key = jax.random.key(seed)
        ks = jax.random.split(key, 8)
        L, D, H, M, B, S = (4, 128, 8, 512, 4, 512)
        std = 0.02
        return {'x': jax.random.normal(ks[0], (B, S, D), dtype=jnp.float32), 'Wq': jax.random.normal(ks[1], (L, D, D), dtype=jnp.float32) * std, 'Wk': jax.random.normal(ks[2], (L, D, D), dtype=jnp.float32) * std, 'Wv': jax.random.normal(ks[3], (L, D, D), dtype=jnp.float32) * std, 'rms_w': jnp.ones((L, H, D // H), dtype=jnp.float32), 'Wo': jax.random.normal(ks[4], (L, D, D), dtype=jnp.float32) * std, 'bo': jnp.zeros((L, D), dtype=jnp.float32), 'diffw': jnp.full((L,), 0.2, dtype=jnp.float32), 'g_ffn': jnp.ones((L, D), dtype=jnp.float32), 'b_ffn': jnp.zeros((L, D), dtype=jnp.float32), 'W1': jax.random.normal(ks[5], (L, M, D), dtype=jnp.float32) * std, 'b1': jnp.zeros((L, M), dtype=jnp.float32), 'W2': jax.random.normal(ks[6], (L, D, M), dtype=jnp.float32) * std, 'b2': jnp.zeros((L, D), dtype=jnp.float32), 'g_f': jnp.ones((D,), dtype=jnp.float32), 'b_f': jnp.zeros((D,), dtype=jnp.float32)}
    _L1_attn_all = _L1_attn_setup()
    _L1_attn_in = {k: v for k, v in _L1_attn_all.items() if k in ('Wq', 'Wk', 'Wv', 'rms_w', 'Wo', 'bo', 'diffw', 'g_ffn', 'b_ffn', 'W1', 'b1', 'W2', 'b2', 'g_f', 'b_f')}
    del _L1_attn_all

    def _L1_ffn_setup():
        import jax, jax.numpy as jnp
        import numpy as np
        IN_FEATURES = 128
        FEATURES = 128
        BATCH, SEQ = (8, 2048)

        def _ste(x_orig, y_proc):
            return x_orig + jax.lax.stop_gradient(y_proc - x_orig)
        key = jax.random.key(seed)
        kx, kw = jax.random.split(key)
        x = jax.random.normal(kx, (BATCH, SEQ, IN_FEATURES), dtype=jnp.float32)
        weight = jax.random.normal(kw, (IN_FEATURES, FEATURES), dtype=jnp.float32) / np.sqrt(IN_FEATURES)
        bias = jnp.zeros((FEATURES,), dtype=jnp.float32)
        return {'x': x, 'weight': weight, 'bias': bias}
    _L1_ffn_all = _L1_ffn_setup()
    _L1_ffn_in = {k: v for k, v in _L1_ffn_all.items() if k in ('weight', 'bias')}
    del _L1_ffn_all
    return {'x': x, 'L0_tok_conv_w': _L0_tok_in['conv_w'], 'L0_attn_source_embedding': _L0_attn_in['source_embedding'], 'L0_attn_value_embedding': _L0_attn_in['value_embedding'], 'L0_attn_Wq': _L0_attn_in['Wq'], 'L0_attn_bq': _L0_attn_in['bq'], 'L0_attn_Wk': _L0_attn_in['Wk'], 'L0_attn_bk': _L0_attn_in['bk'], 'L0_attn_Wv': _L0_attn_in['Wv'], 'L0_attn_bv': _L0_attn_in['bv'], 'L0_attn_Wo': _L0_attn_in['Wo'], 'L0_attn_bo': _L0_attn_in['bo'], 'L0_ffn_and_w1': _L0_ffn_in['and_w1'], 'L0_ffn_and_b1': _L0_ffn_in['and_b1'], 'L0_ffn_and_w2': _L0_ffn_in['and_w2'], 'L0_ffn_and_b2': _L0_ffn_in['and_b2'], 'L0_ffn_or_w1': _L0_ffn_in['or_w1'], 'L0_ffn_or_b1': _L0_ffn_in['or_b1'], 'L0_ffn_or_w2': _L0_ffn_in['or_w2'], 'L0_ffn_or_b2': _L0_ffn_in['or_b2'], 'L0_ffn_xor_w1': _L0_ffn_in['xor_w1'], 'L0_ffn_xor_b1': _L0_ffn_in['xor_b1'], 'L0_ffn_xor_w2': _L0_ffn_in['xor_w2'], 'L0_ffn_xor_b2': _L0_ffn_in['xor_b2'], 'L1_attn_Wq': _L1_attn_in['Wq'], 'L1_attn_Wk': _L1_attn_in['Wk'], 'L1_attn_Wv': _L1_attn_in['Wv'], 'L1_attn_rms_w': _L1_attn_in['rms_w'], 'L1_attn_Wo': _L1_attn_in['Wo'], 'L1_attn_bo': _L1_attn_in['bo'], 'L1_attn_diffw': _L1_attn_in['diffw'], 'L1_attn_g_ffn': _L1_attn_in['g_ffn'], 'L1_attn_b_ffn': _L1_attn_in['b_ffn'], 'L1_attn_W1': _L1_attn_in['W1'], 'L1_attn_b1': _L1_attn_in['b1'], 'L1_attn_W2': _L1_attn_in['W2'], 'L1_attn_b2': _L1_attn_in['b2'], 'L1_attn_g_f': _L1_attn_in['g_f'], 'L1_attn_b_f': _L1_attn_in['b_f'], 'L1_ffn_weight': _L1_ffn_in['weight'], 'L1_ffn_bias': _L1_ffn_in['bias']}

def reference(x, L0_tok_conv_w, L0_attn_source_embedding, L0_attn_value_embedding, L0_attn_Wq, L0_attn_bq, L0_attn_Wk, L0_attn_bk, L0_attn_Wv, L0_attn_bv, L0_attn_Wo, L0_attn_bo, L0_ffn_and_w1, L0_ffn_and_b1, L0_ffn_and_w2, L0_ffn_and_b2, L0_ffn_or_w1, L0_ffn_or_b1, L0_ffn_or_w2, L0_ffn_or_b2, L0_ffn_xor_w1, L0_ffn_xor_b1, L0_ffn_xor_w2, L0_ffn_xor_b2, L1_attn_Wq, L1_attn_Wk, L1_attn_Wv, L1_attn_rms_w, L1_attn_Wo, L1_attn_bo, L1_attn_diffw, L1_attn_g_ffn, L1_attn_b_ffn, L1_attn_W1, L1_attn_b1, L1_attn_W2, L1_attn_b2, L1_attn_g_f, L1_attn_b_f, L1_ffn_weight, L1_ffn_bias):
    import jax
    import jax.numpy as jnp

    def _L0_tok_ref(token_ids, conv_w):
        import jax, jax.numpy as jnp
        import numpy as np
        VOCAB = 8000
        EMB = 128
        K = 3
        B, T = (8, 1024)
        'Equivalent to one_hot(token_ids) -> Conv1d(V->F, k=K, pad=K//2, no bias).\n\n            Because the conv input is one-hot over the vocab channel, the V-dim\n            contraction reduces to gathering one weight row per (position, tap):\n              out[b,t,f] = sum_k W[f, token[b, t+k-pad], k]   (zero outside [0,T)).\n            '
        Bn, Tn = token_ids.shape
        F_, V_, Kn = conv_w.shape
        pad = Kn // 2
        out = jnp.zeros((Bn, Tn, F_), dtype=conv_w.dtype)
        t = jnp.arange(Tn)
        for k in range(Kn):
            shift = k - pad
            src = t + shift
            valid = (src >= 0) & (src < Tn)
            src_c = jnp.clip(src, 0, Tn - 1)
            ids = token_ids[:, src_c]
            table_k = conv_w[:, :, k].T
            emb = table_k[ids]
            out = out + jnp.where(valid[None, :, None], emb, jnp.zeros((), conv_w.dtype))
        return out

    def _L0_attn_ref(target_embedding, source_embedding, value_embedding, Wq, bq, Wk, bk, Wv, bv, Wo, bo):
        import jax, jax.numpy as jnp
        import numpy as np
        D_MODEL, N_HEADS, D_KEYS, D_LLM = (128, 8, 16, 1024)
        B, L, S = (32, 256, 250)
        HE = N_HEADS * D_KEYS
        H, E = (N_HEADS, D_KEYS)
        Bb, Ll, _ = target_embedding.shape
        Ss = source_embedding.shape[0]
        q = (target_embedding @ Wq + bq).reshape(Bb, Ll, H, E)
        k = (source_embedding @ Wk + bk).reshape(Ss, H, E)
        v = (value_embedding @ Wv + bv).reshape(Ss, H, E)
        scale = 1.0 / jnp.sqrt(jnp.asarray(E, q.dtype))
        scores = jnp.einsum('blhe,she->bhls', q, k)
        attn = jax.nn.softmax(scale * scores, axis=-1)
        out = jnp.einsum('bhls,she->blhe', attn, v).reshape(Bb, Ll, H * E)
        return out @ Wo + bo

    def _L0_ffn_ref(x_bd, and_w1, and_b1, and_w2, and_b2, or_w1, or_b1, or_w2, or_b2, xor_w1, xor_b1, xor_w2, xor_b2):
        import jax, jax.numpy as jnp
        import numpy as np
        MARK_AX = 0
        OP_AND = 1
        OP_OR = 2
        OP_XOR = 3
        ALU_LO = 16
        ALU_HI = 32
        AX_CARRY_LO = 48
        AX_CARRY_HI = 64
        OUTPUT_LO = 80
        OUTPUT_HI = 96
        NIB_A = 0
        NIB_B = 1
        OP_START = 16
        RESULT = 64
        GE_DIM = 160
        N_ROWS = 8
        B, S, D = (8, 1024, 128)

        def _decode_nibble(x_bd, start):
            bits = x_bd[..., start:start + 16] > 0.5
            return jnp.argmax(bits, axis=-1).astype(x_bd.dtype)

        def _mlp2(x, w1, b1, w2, b2):
            h = jax.nn.relu(jnp.einsum('bsrd,de->bsre', x, w1) + b1)
            return jnp.einsum('bsrd,de->bsre', h, w2) + b2

        def _forward(x_bd, and_w1, and_b1, and_w2, and_b2, or_w1, or_b1, or_w2, or_b2, xor_w1, xor_b1, xor_w2, xor_b2):
            a_lo = _decode_nibble(x_bd, ALU_LO)
            a_hi = _decode_nibble(x_bd, ALU_HI)
            b_lo = _decode_nibble(x_bd, AX_CARRY_LO)
            b_hi = _decode_nibble(x_bd, AX_CARRY_HI)
            Bsz, Ssz, _ = x_bd.shape
            x_ge = jnp.zeros((Bsz, Ssz, N_ROWS, GE_DIM), x_bd.dtype)
            x_ge = x_ge.at[..., 0, NIB_A].set(a_lo).at[..., 1, NIB_A].set(a_hi)
            x_ge = x_ge.at[..., 0, NIB_B].set(b_lo).at[..., 1, NIB_B].set(b_hi)
            x_ge = x_ge.at[..., :, OP_START + 28].set(x_bd[..., OP_OR, None])
            x_ge = x_ge.at[..., :, OP_START + 29].set(x_bd[..., OP_XOR, None])
            x_ge = x_ge.at[..., :, OP_START + 30].set(x_bd[..., OP_AND, None])
            y_and = _mlp2(x_ge, and_w1, and_b1, and_w2, and_b2)
            y_or = _mlp2(x_ge, or_w1, or_b1, or_w2, or_b2)
            y_xor = _mlp2(x_ge, xor_w1, xor_b1, xor_w2, xor_b2)
            is_and = x_bd[..., OP_AND] > 0.5
            is_or = x_bd[..., OP_OR] > 0.5
            is_xor = x_bd[..., OP_XOR] > 0.5
            sel = jnp.where(is_and[..., None, None], y_and, jnp.where(is_or[..., None, None], y_or, y_xor))
            active = (x_bd[..., MARK_AX] >= 0.5) & (is_and | is_or | is_xor)
            res_lo = jnp.clip(jnp.round(sel[..., 0, RESULT]), 0, 15).astype(jnp.int32)
            res_hi = jnp.clip(jnp.round(sel[..., 1, RESULT]), 0, 15).astype(jnp.int32)
            amask = active.astype(x_bd.dtype)[..., None]
            add_lo = 2.0 * jax.nn.one_hot(res_lo, 16, dtype=x_bd.dtype) * amask
            add_hi = 2.0 * jax.nn.one_hot(res_hi, 16, dtype=x_bd.dtype) * amask
            out = x_bd.at[..., OUTPUT_LO:OUTPUT_LO + 16].add(add_lo)
            out = out.at[..., OUTPUT_HI:OUTPUT_HI + 16].add(add_hi)
            return out
        return _forward(x_bd, and_w1, and_b1, and_w2, and_b2, or_w1, or_b1, or_w2, or_b2, xor_w1, xor_b1, xor_w2, xor_b2)

    def _L1_attn_ref(x, Wq, Wk, Wv, rms_w, Wo, bo, diffw, g_ffn, b_ffn, W1, b1, W2, b2, g_f, b_f):
        import jax, jax.numpy as jnp
        import numpy as np
        LN_EPS = 1e-05
        RMS_EPS = 1.1920929e-07

        def _layernorm(x, g, b):
            m = jnp.mean(x, axis=-1, keepdims=True)
            xc = x - m
            v = jnp.mean(xc * xc, axis=-1, keepdims=True)
            return xc / jnp.sqrt(v + LN_EPS) * g + b

        def layer(xc, p):
            wq, wk, wv, rw, wo, bob, dw, g1, bn1, w1, bb1, w2, bb2 = p
            B, S, D = xc.shape
            H = rw.shape[0]
            F = D // (2 * H)
            qs = (xc @ wq.T).reshape(B, S, H, 2, F)
            ks_ = (xc @ wk.T).reshape(B, S, H, 2, F)
            scores = jnp.einsum('bqhif,bkhif->ibhqk', qs, ks_) * F ** (-0.5)
            atts = jax.nn.softmax(scores, axis=-1)
            att = atts[0] - dw * atts[1]
            vs = (xc @ wv.T).reshape(B, S, H, D // H)
            o = jnp.einsum('bhqk,bkhe->bqhe', att, vs)
            o = o / jnp.sqrt(jnp.mean(o * o, axis=(-2, -1), keepdims=True) + RMS_EPS) * rw
            xa = (o.reshape(B, S, D) @ wo.T + bob) * (1.0 - dw)
            xc = xa + xc
            h = _layernorm(xc, g1, bn1)
            h = jax.nn.gelu(h @ w1.T + bb1, approximate=False)
            xc = h @ w2.T + bb2 + xc
            return (xc, None)
        xf, _ = jax.lax.scan(layer, x, (Wq, Wk, Wv, rms_w, Wo, bo, diffw, g_ffn, b_ffn, W1, b1, W2, b2))
        return _layernorm(xf, g_f, b_f)

    def _L1_ffn_ref(x, weight, bias):
        import jax, jax.numpy as jnp
        import numpy as np
        IN_FEATURES = 128
        FEATURES = 128
        BATCH, SEQ = (8, 2048)

        def _ste(x_orig, y_proc):
            return x_orig + jax.lax.stop_gradient(y_proc - x_orig)
        weight_centered = weight - jnp.mean(weight)
        weight_bin = jnp.sign(weight_centered)
        weight_bin_ste = _ste(weight, weight_bin)
        scale_gamma = jnp.mean(jnp.abs(weight))
        effective_weight = weight_bin_ste * scale_gamma
        y = jnp.dot(x, effective_weight) + bias
        act_clipped = jnp.clip(y, -1.0, 1.0)
        quant_dequant = jnp.round(act_clipped * 7.0) / 7.0
        return _ste(y, quant_dequant)
    h = _L0_tok_ref(x, L0_tok_conv_w)
    h = h + _L0_attn_ref(_layernorm(h, axis=-1), L0_attn_source_embedding, L0_attn_value_embedding, L0_attn_Wq, L0_attn_bq, L0_attn_Wk, L0_attn_bk, L0_attn_Wv, L0_attn_bv, L0_attn_Wo, L0_attn_bo)
    h = h + _L0_ffn_ref(_layernorm(h, axis=-1), L0_ffn_and_w1, L0_ffn_and_b1, L0_ffn_and_w2, L0_ffn_and_b2, L0_ffn_or_w1, L0_ffn_or_b1, L0_ffn_or_w2, L0_ffn_or_b2, L0_ffn_xor_w1, L0_ffn_xor_b1, L0_ffn_xor_w2, L0_ffn_xor_b2)
    h = h + _L1_attn_ref(_layernorm(h, axis=-1), L1_attn_Wq, L1_attn_Wk, L1_attn_Wv, L1_attn_rms_w, L1_attn_Wo, L1_attn_bo, L1_attn_diffw, L1_attn_g_ffn, L1_attn_b_ffn, L1_attn_W1, L1_attn_b1, L1_attn_W2, L1_attn_b2, L1_attn_g_f, L1_attn_b_f)
    h = h + _L1_ffn_ref(_layernorm(h, axis=-1), L1_ffn_weight, L1_ffn_bias)
    return h

_drawn_inputs = setup_inputs


def setup_inputs(seed=0):
    import zlib

    import numpy as np

    out = dict(_drawn_inputs(seed))
    spreads = {'L0_attn_bq': (0.0, 0.542),
     'L0_attn_bk': (0.0, 2.0),
     'L0_attn_bv': (0.0, 0.1),
     'L0_attn_bo': (0.0, 0.1),
     'L0_ffn_and_b1': (0.0, 0.1),
     'L0_ffn_and_b2': (0.0, 0.1),
     'L0_ffn_or_b1': (0.0, 2.0),
     'L0_ffn_or_b2': (0.0, 2.0),
     'L0_ffn_xor_b1': (0.0, 0.8),
     'L0_ffn_xor_b2': (0.0, 0.1),
     'L1_attn_rms_w': (1.0, 0.2),
     'L1_attn_bo': (0.0, 0.1),
     'L1_attn_diffw': (0.20000000298023224, 0.6),
     'L1_attn_g_ffn': (1.0, 0.6),
     'L1_attn_b_ffn': (0.0, 0.8),
     'L1_attn_b1': (0.0, 0.294),
     'L1_attn_b2': (0.0, 0.1),
     'L1_attn_g_f': (1.0, 0.2),
     'L1_attn_b_f': (0.0, 0.1),
     'L1_ffn_bias': (0.0, 0.1)}
    factors = {'L0_ffn_or_w1': 21.663,
     'L0_ffn_or_w2': 24.22,
     'L0_ffn_xor_w2': 8.0,
     'L1_attn_Wq': 26.781,
     'L1_attn_Wk': 28.016,
     'L0_ffn_xor_w1': 2.723}
    for name, (base, spread) in spreads.items():
        noise = np.random.default_rng([zlib.crc32(name.encode()), seed]).standard_normal(out[name].shape)
        drawn = base * np.exp(spread * noise) if base else spread * noise
        out[name] = jnp.asarray(drawn.astype(out[name].dtype))
    for name, factor in factors.items():
        out[name] = (out[name] * factor).astype(out[name].dtype)
    return out
```

```python
from contextlib import ExitStack
import numpy as np
import concourse.bass as bass
from concourse import mybir

F32 = mybir.dt.float32
BF16 = mybir.dt.bfloat16
I32 = mybir.dt.int32
ACT = mybir.ActivationFunctionType
ALU = mybir.AluOpType
AX = mybir.AxisListType

P = 128
D = 128
SEQS = 16
TOK = 512
QT = TOK // P
LAYERS = 4
ITEMS = LAYERS * SEQS

HEADS = 8
GROUPS = 2 * HEADS
F = D // GROUPS
E = D // HEADS
VW = 32
QUADS = GROUPS // 4
STEPS = GROUPS
PARTS = 3
COMBOS = 6
Q_PART = (0, 0, 0, 1, 1, 2)
K_PART = (0, 1, 2, 0, 1, 0)
CROWS = COMBOS * F
MROWS = CROWS + PARTS
SCALE = float(F) ** -0.5
RMS_EPS = 1.1920929e-07
LN_EPS = 1e-05
HID = 512
HT = HID // P

WO0, W10, W20 = 0, D, D + HID
RW0 = D + 2 * HID
G0, B0, B10, DW0, BO0, B20 = RW0 + 1, RW0 + 2, RW0 + 3, RW0 + 3 + HT, RW0 + 4 + HT, RW0 + 4 + HT + D
TPAR = B20 + D


def count(value):
    return max(value, 0) if isinstance(value, int) else value


def blocks(nc, w_qk, w_v, w_tail, ident_d, x_hist, scr_q, scr_k, scr_m):
    with ExitStack() as ctx:
        def sb(name, shape, dt=F32):
            return ctx.enter_context(nc.sbuf_tensor(name, shape, dt))

        def ps(name, shape):
            return ctx.enter_context(nc.psum_tensor(name, shape, F32))

        def sem(name):
            return ctx.enter_context(nc.semaphore(name))

        ident = sb("bl_ident", [P, P])
        q_ops = [sb(f"q_ops{i}", [64, GROUPS, TOK], BF16) for i in range(2)]
        k_ops = [sb(f"k_ops{i}", [64, GROUPS, TOK], BF16) for i in range(2)]
        v_ops = [sb(f"v_ops{i}", [P, QT, HEADS, VW]) for i in range(2)]
        probs = sb("probs", [P, 4, 4, TOK])
        wqk = sb("wqk", [P, 2, D])
        wv = sb("wv", [P, D])
        xs = sb("xs", [P, QT, D])
        xT = sb("xT", [P, TOK])
        parts = sb("parts", [P, 2, PARTS, TOK], BF16)
        rest = sb("rest", [P, 2, TOK])
        mx = sb("mx", [P, 2, 16])
        m_parts = sb("m_parts", [16, 2, PARTS, P], BF16)
        m_rest = sb("m_rest", [16, 2, P])
        oT_raw = sb("oT_raw", [P, 2, TOK])
        rz = sb("rz", [P, 2, QT, 4])
        o_norm = sb("o_norm", [P, QT * HEADS, 2, E])
        o_neg = sb("o_neg", [P, QT * HEADS, E])
        o_tok = sb("o_tok", [P, QT, D])
        junk = sb("junk", [P, QT, D])
        sumsq = sb("sumsq", [P, QT])
        rms = sb("rms", [P, QT])
        half = sb("half", [P, QT])
        omd = sb("omd", [P, 1])
        ndw = sb("ndw", [P, 1])
        bos = sb("bos", [P, D])
        xt = sb("xt", [P, QT, D])
        xb = sb("xb", [P, QT, D])
        x1 = sb("x1", [P, QT, D])
        x1b = sb("x1b", [P, QT, D])
        x2 = sb("x2", [P, QT, D])
        stats = sb("stats", [P, QT, 6])
        mv = sb("mv", [P, QT, 2])
        rstd = sb("rstd", [P, QT])
        xn = sb("xn", [P, QT, D])
        oT = sb("oT", [P, TOK])
        hT = sb("hT", [P, TOK])
        u_in = sb("u_in", [P, HT, TOK])
        u = sb("u", [P, HT, TOK])
        wt = sb("wt", [P, TPAR])

        st_ps = [ps(f"st_ps{i}", [P, TOK]) for i in range(3)]
        s_ps = [ps(f"s_ps{i}", [P, TOK]) for i in range(2)]
        o_ps = ps("o_ps", [P, TOK])
        tail_ps = ps("tail_ps", [P, TOK])
        proj_ps = ps("proj_ps", [P, TOK])
        tail3 = tail_ps[:, :].rearrange("p (a b) -> p a b", a=QT)
        proj3 = proj_ps[:, :].rearrange("p (a b) -> p a b", a=QT)

        names = """const_ready half_ready ident_loaded ones_ready
            st_ready exp_done pv_done o_copied oq_ready rz_done oq_taken
            s_ready s_taken mxt_ready m1_done mr_done m2_done m3_done m_written
            wqk_loaded wv_loaded xs_loaded xt_ready xt_done q_ready k_ready q1_done k1_done qr_done kr_done
            q2_done k2_done q3_done k3_done qk_written v_ready v_done
            t_loaded omd_done bos_done xb_done neg_done o_done sq_done ms_done pow_done rms_done
            ot_ready ot_done wo_ready x1_done bn_done mv_done ve_done rs_done xn_done x1b_done ht_ready ht_done
            w1_ready u_in_done gelu_done w2_ready x2_done x_stored""".split()
        S = {n: sem(n) for n in names}
        op_loaded = [sem(f"op_loaded{q}") for q in range(QUADS)]
        m_loaded = [sem(f"m_loaded{q}") for q in range(QUADS)]
        (const_ready, half_ready, ident_loaded, ones_ready,
         st_ready, exp_done, pv_done, o_copied, oq_ready, rz_done, oq_taken,
         s_ready, s_taken, mxt_ready, m1_done, mr_done, m2_done, m3_done, m_written,
         wqk_loaded, wv_loaded, xs_loaded, xt_ready, xt_done, q_ready, k_ready, q1_done, k1_done, qr_done, kr_done,
         q2_done, k2_done, q3_done, k3_done, qk_written, v_ready, v_done,
         t_loaded, omd_done, bos_done, xb_done, neg_done, o_done, sq_done, ms_done, pow_done, rms_done,
         ot_ready, ot_done, wo_ready, x1_done, bn_done, mv_done, ve_done, rs_done, xn_done, x1b_done, ht_ready, ht_done,
         w1_ready, u_in_done, gelu_done, w2_ready, x2_done, x_stored) = [S[n] for n in names]
        block = ctx.enter_context(nc.Block())

        def walk(eng, item):
            for i in range(2):
                item(i, i)
            with eng.Fori(1, ITEMS // 2 - 1) as pair:
                for par in range(2):
                    item(pair * 2 + par, par, inner=True)
            for i in range(ITEMS - 2, ITEMS):
                item(i, i % 2)

        def st_bank(par, s, j):
            return (par * 64 + 4 * s + j) % 3

        def runs(it, inner):
            if inner:
                return True, True, True, True
            return it >= 1, it >= 2, it + 1 < ITEMS, it + 2 < ITEMS

        @block.sync
        def _(sp):
            def load_projection_inputs(ip):
                sp.wait_ge(xt_ready, ip)
                sp.nop(nofuse=True)
                sp.dma_start(xs[:], x_hist[ip].rearrange("p (a b) -> p a b", a=QT)).then_inc(xs_loaded, 16)
                sp.wait_ge(k_ready, ip)
                sp.nop(nofuse=True)
                sp.dma_start(wqk[:], w_qk[ip // SEQS]).then_inc(wqk_loaded, 16)

            def load_value_weights(iv):
                sp.wait_ge(v_ready, iv)
                sp.nop(nofuse=True)
                sp.dma_start(wv[:], w_v[iv // SEQS]).then_inc(wv_loaded, 16)

            def stage_operands(ip, par):
                for q in range(QUADS):
                    sp.wait_ge(op_loaded[q], count(32 * (ip - 1)))
                    sp.nop(nofuse=True)
                for done, which, scr, part in ((q3_done, 0, scr_q, Q_PART), (k3_done, 1, scr_k, K_PART)):
                    sp.wait_ge(done, ip + 1)
                    sp.nop(nofuse=True)
                    for c in range(COMBOS):
                        sp.dma_start(scr[par, c], parts[:, which, part[c], :]).then_inc(qk_written, 16)
                sp.wait_ge(qk_written, 2 * COMBOS * 16 * (ip + 1))
                sp.nop(nofuse=True)

            def load_operands(ip, par, q):
                sp.wait_ge(st_ready, count((ip - 2) * 64 + 16 * (q + 1)))
                sp.nop(nofuse=True)
                for ops, scr in ((q_ops, scr_q), (k_ops, scr_k)):
                    src = scr[par].rearrange("c (d g) t -> (c d) g t", g=GROUPS)[:, 4 * q:4 * q + 4, :]
                    sp.dma_start(ops[par][0:CROWS, 4 * q:4 * q + 4, :], src).then_inc(op_loaded[q], 16)

            def move_maxima(im, par, q):
                sp.wait_ge(m3_done, im * 4 + q + 1)
                sp.nop(nofuse=True)
                sp.dma_start(scr_m[par, q].rearrange("c p t -> p c t"), m_parts[:, q % 2, :, :]).then_inc(m_written, 16)
                sp.wait_ge(m_written, 16 * (im * 4 + q + 1))
                sp.nop(nofuse=True)
                sp.wait_ge(st_ready, count((im - 2) * 64 + 16 * (q + 1)))
                sp.nop(nofuse=True)
                sp.dma_start(q_ops[par][CROWS:MROWS, 4 * q:4 * q + 4, :],
                             scr_m[par, q].rearrange("c (g a) t -> c g (a t)", g=4)).then_inc(m_loaded[q], 16)

            def store_x(itt):
                sp.wait_ge(x2_done, itt + 1)
                sp.nop(nofuse=True)
                sp.dma_start(x_hist[itt + SEQS], x2[:].rearrange("p a b -> p (a b)")).then_inc(x_stored, 16)

            def load_tail_inputs(itt):
                sp.dma_start(xt[:], x_hist[itt].rearrange("p (a b) -> p a b", a=QT)).then_inc(t_loaded, 16)
                sp.dma_start(wt[:], w_tail[itt // SEQS]).then_inc(t_loaded, 16)

            def item(it, par, inner=False):
                tail, tail_end, maxima, projections = runs(it, inner)
                if tail_end:
                    store_x(it - 2)
                if tail:
                    load_tail_inputs(it - 1)
                if maxima:
                    load_value_weights(it + 1)
                if tail_end:
                    sp.wait_ge(x_stored, count(16 * (it - 1)))
                    sp.nop(nofuse=True)
                if projections:
                    load_projection_inputs(it + 2)
                move_maxima(it, par, 3)
                if maxima:
                    move_maxima(it + 1, 1 - par, 0)
                if projections:
                    stage_operands(it + 2, par)
                    load_operands(it + 2, par, 0)
                if maxima:
                    move_maxima(it + 1, 1 - par, 1)
                if projections:
                    load_operands(it + 2, par, 1)
                    load_operands(it + 2, par, 2)
                if maxima:
                    move_maxima(it + 1, 1 - par, 2)
                if projections:
                    load_operands(it + 2, par, 3)

            sp.dma_start(ident[:], ident_d).then_inc(ident_loaded, 16)
            sp.wait_ge(ones_ready, 4)
            sp.nop(nofuse=True)
            for ip in range(2):
                load_value_weights(ip) if ip == 0 else None
                load_projection_inputs(ip)
                stage_operands(ip, ip)
                for q in range(QUADS):
                    load_operands(ip, ip, q)
            for q in range(QUADS - 1):
                move_maxima(0, 0, q)
            walk(sp, item)
            store_x(ITEMS - 2)
            load_tail_inputs(ITEMS - 1)
            store_x(ITEMS - 1)
            sp.wait_ge(x_stored, 16 * ITEMS)
            sp.nop(nofuse=True)

        @block.tensor
        def _(pe):
            mm, tr = nc.tensor.matmul, nc.tensor.transpose

            def score_t(it, par, s, j):
                g, kt = 4 * (s // 4) + j, s % 4
                t = it * 64 + 4 * s + j
                if kt == 0 and j == 0:
                    pe.wait_ge(m_loaded[s // 4], 16 * (it + 1))
                pe.wait_ge(exp_done, count(t - 1 if par == 0 and s == 0 and j < 2 else t - 2))
                mm(st_ps[st_bank(par, s, j)][:], k_ops[par][0:MROWS, g, kt * P:(kt + 1) * P], q_ops[par][0:MROWS, g, :],
                   start=True, stop=True).then_inc(st_ready, 1)

            def score(im, par, g, qt):
                if qt == 0 and g % 4 == 0:
                    pe.wait_ge(op_loaded[g // 4], 32 * (im + 1))
                pe.wait_ge(s_taken, count(im * 64 + 4 * g + qt - 1))
                mm(s_ps[qt % 2][:], q_ops[par][0:CROWS, g, qt * P:(qt + 1) * P], k_ops[par][0:CROWS, g, :],
                   start=True, stop=True).then_inc(s_ready, 1)

            def weigh_values(n_it, par, s):
                q, kt = s // 4, s % 4
                pe.wait_ge(exp_done, n_it * 64 + 4 * s + 4)
                if s == 0:
                    pe.wait_ge(v_done, n_it + 1)
                if kt == 0:
                    pe.wait_ge(o_copied, n_it * 4 + q)
                for j in range(4):
                    last = mm(o_ps[32 * j:32 * j + VW, :], v_ops[par][:, kt, (4 * q + j) // 2, :],
                              probs[:, s % 4, j, :], start=kt == 0, stop=kt == 3)
                last.then_inc(pv_done, 1)

            def turn_quad(it, q, free, value):
                pe.wait_ge(o_copied, it * 4 + q + 1)
                pe.wait_ge(free, count(value))
                for a in range(QT):
                    last = tr(tail3[:, a, :], oT_raw[:, q % 2, a * P:(a + 1) * P], ident[:])
                last.then_inc(oq_ready, 1)

            def turn_maxima(im, q, free, value):
                pe.wait_ge(s_taken, im * 64 + 16 * (q + 1))
                pe.wait_ge(free, count(value))
                tr(proj_ps[0:16, 0:P], mx[:, q % 2, :], ident[:]).then_inc(mxt_ready, 1)

            def values(iv):
                pe.wait_ge(xt_done, iv + 1)
                pe.wait_ge(wv_loaded, 16 * (iv + 1))
                pe.wait_ge(mr_done, iv * 4)
                for a in range(QT):
                    last = mm(proj3[:, a, :], xT[:, a * P:(a + 1) * P], wv[:], start=True, stop=True)
                last.then_inc(v_ready, 1)

            def turn_x(ip):
                pe.wait_ge(xs_loaded, 16 * (ip + 1))
                pe.wait_ge(v_done, ip)
                for a in range(QT):
                    last = tr(proj3[:, a, :], xs[:, a, :], ident[:])
                last.then_inc(xt_ready, 1)

            def project(ip, which, free, value):
                if which == 0:
                    pe.wait_ge(wqk_loaded, 16 * (ip + 1))
                    pe.wait_ge(xt_done, ip + 1)
                pe.wait_ge(free, count(value))
                mm(proj_ps[:], wqk[:, which, :], xT[:], start=True, stop=True).then_inc((q_ready, k_ready)[which], 1)

            def turn_o(itt):
                pe.wait_ge(o_done, itt + 1)
                pe.wait_ge(oq_taken, 4 * (itt + 1))
                for a in range(QT):
                    last = tr(tail3[:, a, :], o_tok[:, a, :], ident[:])
                last.then_inc(ot_ready, 1)

            def project_o(itt):
                pe.wait_ge(t_loaded, 32 * (itt + 1))
                pe.wait_ge(ot_done, itt + 1)
                for a in range(QT):
                    last = mm(tail3[:, a, :], oT[:, a * P:(a + 1) * P], wt[:, WO0:WO0 + D], start=True, stop=True)
                last.then_inc(wo_ready, 1)

            def turn_h(itt, free, value):
                pe.wait_ge(xn_done, QT * (itt + 1))
                pe.wait_ge(free, count(value))
                for a in range(QT):
                    last = tr(tail3[:, a, :], xn[:, a, :], ident[:])
                last.then_inc(ht_ready, 1)

            def up(itt, j, free, value):
                if j == 0:
                    pe.wait_ge(ht_done, itt + 1)
                pe.wait_ge(free, count(value))
                mm(tail_ps[:], wt[:, W10 + j * P:W10 + (j + 1) * P], hT[:], start=True, stop=True).then_inc(w1_ready, 1)

            def down(itt, free, value):
                pe.wait_ge(gelu_done, itt + 1)
                pe.wait_ge(free, count(value))
                for a in range(QT):
                    for j in range(HT):
                        last = mm(tail3[:, a, :], u[:, j, a * P:(a + 1) * P], wt[:, W20 + j * P:W20 + (j + 1) * P],
                                  start=j == 0, stop=j == HT - 1)
                last.then_inc(w2_ready, 1)

            def tail_alone(itt):
                turn_quad(itt, 2, x2_done, itt)
                turn_quad(itt, 3, oq_taken, itt * 4 + 3)
                turn_o(itt)
                project_o(itt)
                turn_h(itt, x1_done, itt + 1)
                for j in range(HT):
                    up(itt, j, u_in_done if j else ht_done, HT * itt + j if j else itt + 1)
                down(itt, u_in_done, HT * (itt + 1))

            def between(it, par, s, tail, maxima, projections):
                if s == 0:
                    turn_maxima(it, 3, mr_done, it * 4 + 3)
                    if tail:
                        turn_quad(it - 1, 2, x2_done, it - 1)
                if s == 1 and tail:
                    turn_quad(it - 1, 3, oq_taken, it * 4 - 1)
                if s == 2 and maxima:
                    values(it + 1)
                if s == 3 and tail:
                    turn_o(it - 1)
                if s == 4:
                    if tail:
                        project_o(it - 1)
                    if projections:
                        turn_x(it + 2)
                if s == 5 and maxima:
                    turn_maxima(it + 1, 0, xt_done if projections else v_done, it + 3 if projections else it + 2)
                if s == 6:
                    turn_quad(it, 0, x1_done if tail else oq_taken, it)
                if s == 7 and projections:
                    project(it + 2, 0, mr_done, it * 4 + 5)
                if s == 9:
                    turn_quad(it, 1, oq_taken, it * 4 + 1)
                    if projections:
                        project(it + 2, 1, qr_done, it + 3)
                if s == 10 and tail:
                    turn_h(it - 1, oq_taken, it * 4 + 2)
                if s == 11:
                    if tail:
                        up(it - 1, 0, ht_done, it)
                    if maxima:
                        turn_maxima(it + 1, 1, kr_done if projections else mr_done,
                                    it + 3 if projections else it * 4 + 5)
                if s in (12, 13, 14) and tail:
                    up(it - 1, s - 11, u_in_done, it * 4 - 15 + s)
                if s == 13 and maxima:
                    turn_maxima(it + 1, 2, mr_done, it * 4 + 6)

            def item(it, par, inner=False):
                tail, tail_end, maxima, projections = runs(it, inner)
                for s in range(STEPS):
                    last = s == STEPS - 1
                    if maxima:
                        score(it + 1, 1 - par, s, 0)
                    score_t(it, par, s, 0)
                    score_t(it, par, s, 1)
                    if maxima:
                        score(it + 1, 1 - par, s, 1)
                    score_t(it, par, s, 2)
                    if not last:
                        score_t(it, par, s, 3)
                    if maxima:
                        score(it + 1, 1 - par, s, 2)
                    between(it, par, s, tail, maxima, projections)
                    if s > 0:
                        weigh_values(it, par, s - 1)
                    elif tail:
                        weigh_values(it - 1, 1 - par, STEPS - 1)
                    if maxima:
                        score(it + 1, 1 - par, s, 3)
                    if last:
                        if tail:
                            down(it - 1, u_in_done, it * 4)
                        score_t(it, par, s, 3)

            pe.wait_ge(ident_loaded, 16)
            for ip in range(2):
                turn_x(ip) if ip == 0 else None
                if ip == 1:
                    pe.wait_ge(kr_done, 1)
                    values(0)
                    turn_x(1)
                project(ip, 0, kr_done, ip)
                project(ip, 1, qr_done, ip + 1)
            for q in range(QUADS):
                for g in range(4 * q, 4 * q + 4):
                    for a in range(QT):
                        score(0, 0, g, a)
                if q < QUADS - 1:
                    turn_maxima(0, q, kr_done if q == 0 else mr_done, 2 if q == 0 else q)
            walk(pe, item)
            weigh_values(ITEMS - 1, 1, STEPS - 1)
            tail_alone(ITEMS - 1)

        @block.scalar
        def _(act):
            A = nc.scalar.activation

            def exps(it, par, s, j):
                t = it * 64 + 4 * s + j
                act.wait_ge(st_ready, t + 1)
                if j == 0:
                    act.wait_ge(pv_done, count(it * 16 + s - 3))
                A(probs[:, s % 4, j, :], st_ps[st_bank(par, s, j)][:], ACT.Exp, scale=SCALE).then_inc(exp_done, 1)

            def copy_quad(it, q):
                act.wait_ge(pv_done, it * 16 + 4 * (q + 1))
                act.wait_ge(oq_ready, count(it * 4 + q - 1))
                nc.scalar.copy(oT_raw[:, q % 2, :], o_ps[:]).then_inc(o_copied, 1)

            def m_first(im, q):
                act.wait_ge(mxt_ready, im * 4 + q + 1)
                act.wait_ge(m_written, count(16 * (im * 4 + q - 1)))
                A(m_parts[:, q % 2, 0, :], proj_ps[0:16, 0:P], ACT.Copy, scale=-1.0).then_inc(m1_done, 1)

            def m_second(im, q):
                act.wait_ge(mr_done, im * 4 + q + 1)
                nc.scalar.copy(m_parts[:, q % 2, 1, :], m_rest[:, q % 2, :]).then_inc(m2_done, 1)

            def copy_x(ip):
                act.wait_ge(xt_ready, ip + 1)
                act.wait_ge(v_ready, ip)
                act.wait_ge(k_ready, ip)
                nc.scalar.copy(xT[:], proj_ps[:]).then_inc(xt_done, 1)

            def first_part(ip, which):
                act.wait_ge((q_ready, k_ready)[which], count(ip + 1))
                act.wait_ge(qk_written, 2 * COMBOS * 16 * ip)
                nc.scalar.copy(parts[:, which, 0, :], proj_ps[:]).then_inc((q1_done, k1_done)[which], 1)

            def second_part(ip, which):
                act.wait_ge((qr_done, kr_done)[which], count(ip + 1))
                nc.scalar.copy(parts[:, which, 1, :], rest[:, which, :]).then_inc((q2_done, k2_done)[which], 1)

            def squares(itt):
                act.wait_ge(o_done, itt + 1)
                act.wait_ge(sq_done, QT * itt)
                act.wait_ge(ms_done, itt)
                for a in range(QT):
                    A(junk[:, a, :], o_tok[:, a, :], ACT.Square, accum_out=sumsq[:, a:a + 1]).then_inc(sq_done, 1)

            def scale_o(itt):
                act.wait_ge(ot_ready, itt + 1)
                act.wait_ge(t_loaded, 32 * (itt + 1))
                A(oT[:], tail_ps[:], ACT.Copy, scale=wt[:, RW0:RW0 + 1]).then_inc(ot_done, 1)

            def affine_h(itt):
                act.wait_ge(ht_ready, itt + 1)
                A(hT[:], tail_ps[:], ACT.Identity, scale=wt[:, G0:G0 + 1], bias=wt[:, B0:B0 + 1]).then_inc(ht_done, 1)

            def hidden(itt, j):
                act.wait_ge(w1_ready, HT * itt + j + 1)
                if j == 0:
                    act.wait_ge(gelu_done, itt)
                A(u_in[:, j, :], tail_ps[:], ACT.Identity, bias=wt[:, B10 + j:B10 + j + 1]).then_inc(u_in_done, 1)

            def gelus(itt):
                act.wait_ge(u_in_done, HT * (itt + 1))
                act.wait_ge(w2_ready, itt)
                A(u[:], u_in[:], ACT.Gelu).then_inc(gelu_done, 1)

            def item(it, par, inner=False):
                tail, tail_end, maxima, projections = runs(it, inner)
                for s in range(STEPS):
                    exps(it, par, s, 0)
                    if s == 1 and tail:
                        copy_quad(it - 1, 3)
                    if s == 4 and tail:
                        scale_o(it - 1)
                    if s in (5, 9, 13):
                        copy_quad(it, s // 4 - 1)
                    for j in range(1, 4):
                        exps(it, par, s, j)
                    if s == 0:
                        m_first(it, 3)
                    if s == 1:
                        m_second(it, 3)
                    if s == 3 and tail:
                        squares(it - 1)
                    if s == 4 and projections:
                        copy_x(it + 2)
                    if s == 5 and maxima:
                        m_first(it + 1, 0)
                    if s == 6 and maxima:
                        m_second(it + 1, 0)
                    if s == 7 and projections:
                        first_part(it + 2, 0)
                    if s == 8 and projections:
                        second_part(it + 2, 0)
                    if s == 9 and projections:
                        first_part(it + 2, 1)
                    if s == 10:
                        if tail:
                            affine_h(it - 1)
                        if projections:
                            second_part(it + 2, 1)
                    if s in (11, 13) and maxima:
                        m_first(it + 1, s // 2 - 4)
                    if s in (11, 12, 13, 14) and tail:
                        hidden(it - 1, s - 11)
                    if s in (12, 14) and maxima:
                        m_second(it + 1, s // 2 - 5)
                    if s == 14 and tail:
                        gelus(it - 1)

            for ip in range(2):
                copy_x(ip)
                for which in range(2):
                    first_part(ip, which)
                    second_part(ip, which)
            for q in range(QUADS - 1):
                m_first(0, q)
                m_second(0, q)
            walk(act, item)
            last = ITEMS - 1
            copy_quad(last, 3)
            squares(last)
            scale_o(last)
            affine_h(last)
            for j in range(HT):
                hidden(last, j)
            gelus(last)

        @block.vector
        def _(dve):
            V = nc.vector

            def maximum(im, g, qt):
                t = im * 64 + 4 * g + qt
                dve.wait_ge(s_ready, t + 1)
                if g % 4 == 0 and qt == 0:
                    dve.wait_ge(mxt_ready, count(im * 4 + g // 4 - 1))
                c = 4 * (g % 4) + qt
                V.reduce_max(mx[:, (g // 4) % 2, c:c + 1], s_ps[qt % 2][:], AX.X).then_inc(s_taken, 1)

            def m_remainder(im, q):
                dve.wait_ge(m1_done, im * 4 + q + 1)
                dve.wait_ge(m3_done, count(im * 4 + q - 1))
                V.scalar_tensor_tensor(out=m_rest[:, q % 2, :], in0=proj_ps[0:16, 0:P], scalar=-1.0,
                                       in1=m_parts[:, q % 2, 0, :], op0=ALU.mult, op1=ALU.subtract).then_inc(mr_done, 1)

            def remainder(ip, which):
                dve.wait_ge((q1_done, k1_done)[which], count(ip + 1))
                dve.wait_ge((q3_done, k3_done)[which], count(ip))
                V.tensor_tensor(rest[:, which, :], proj_ps[:], parts[:, which, 0, :],
                                ALU.subtract).then_inc((qr_done, kr_done)[which], 1)

            def keep_values(iv, par):
                dve.wait_ge(v_ready, iv + 1)
                dve.wait_ge(pv_done, count(16 * (iv - 1)))
                V.tensor_copy(v_ops[par][:, :, :, 0:E],
                              proj_ps[:].rearrange("p (a h e) -> p a h e", a=QT, h=HEADS)).then_inc(v_done, 1)

            def normalise(it, q):
                src = tail_ps[:].rearrange("p (a j w) -> p a j w", a=QT, j=4)
                dve.wait_ge(oq_ready, it * 4 + q + 1)
                V.reciprocal(rz[:, q % 2, :, :], src[:, :, :, E]).then_inc(rz_done, 1)
                dve.wait_ge(rz_done, it * 4 + q + 1)
                if q == 0:
                    dve.wait_ge(o_done, it)
                dst = o_norm[:].rearrange("p (a q h) i e -> p a q (h i) e", a=QT, q=QUADS)[:, :, q]
                V.tensor_tensor(dst, src[:, :, :, 0:E], rz[:, q % 2, :, :].unsqueeze(3).to_broadcast([P, QT, 4, E]),
                                ALU.mult).then_inc(oq_taken, 1)

            def add_attention(itt):
                dve.wait_ge(wo_ready, itt + 1)
                dve.wait_ge(rms_done, itt + 1)
                dve.wait_ge(xb_done, itt + 1)
                dve.wait_ge(x1b_done, itt)
                dve.wait_ge(xn_done, QT * itt)
                for a in range(QT):
                    last = V.scalar_tensor_tensor(out=x1[:, a, :], in0=tail3[:, a, :], scalar=rms[:, a:a + 1],
                                                  in1=xb[:, a, :], op0=ALU.mult, op1=ALU.add)
                last.then_inc(x1_done, 1)

            def statistics(itt):
                dve.wait_ge(x1_done, itt + 1)
                for a in range(QT):
                    last = V.bn_stats(stats[:, a, :], x1[:, a, :])
                last.then_inc(bn_done, 1)
                dve.wait_ge(bn_done, itt + 1)
                dve.nop(nofuse=True)
                for a in range(QT):
                    last = V.bn_aggr(mv[:, a, :], stats[:, a, :])
                last.then_inc(mv_done, 1)

            def add_mlp(itt):
                dve.wait_ge(w2_ready, itt + 1)
                dve.wait_ge(x1b_done, itt + 1)
                dve.wait_ge(x_stored, 16 * itt)
                V.tensor_tensor(x2[:], tail3[:], x1b[:], ALU.add).then_inc(x2_done, 1)

            def item(it, par, inner=False):
                tail, tail_end, maxima, projections = runs(it, inner)
                for s in range(STEPS):
                    if maxima:
                        for j in range(3):
                            maximum(it + 1, s, j)
                    if s == 0 and tail:
                        normalise(it - 1, 2)
                    if s == 1:
                        m_remainder(it, 3)
                        if tail:
                            normalise(it - 1, 3)
                    if s == 2 and maxima:
                        keep_values(it + 1, 1 - par)
                    if s == 5 and tail:
                        add_attention(it - 1)
                    if s == 6:
                        if tail:
                            statistics(it - 1)
                        if maxima:
                            m_remainder(it + 1, 0)
                    if s == 7:
                        normalise(it, 0)
                    if s == 8 and projections:
                        remainder(it + 2, 0)
                    if s == 9:
                        normalise(it, 1)
                    if s == 10 and projections:
                        remainder(it + 2, 1)
                    if s in (12, 14) and maxima:
                        m_remainder(it + 1, s // 2 - 5)
                    if maxima:
                        maximum(it + 1, s, 3)
                if tail:
                    add_mlp(it - 1)

            for i in range(2):
                V.memset(k_ops[i][32:64, :, :], 1.0).then_inc(ones_ready, 1)
                V.memset(q_ops[i][32:64, :, :], 0.0).then_inc(ones_ready, 1)
                V.memset(v_ops[i][:], 0.0).then_inc(const_ready, 1)
            dve.wait_ge(const_ready, 2)
            for i in range(2):
                V.memset(v_ops[i][:, :, :, E:E + 1], 1.0).then_inc(const_ready, 1)
            dve.wait_ge(const_ready, 4)
            for ip in range(2):
                if ip == 1:
                    keep_values(0, 0)
                remainder(ip, 0)
                remainder(ip, 1)
            for q in range(QUADS):
                for g in range(4 * q, 4 * q + 4):
                    for a in range(QT):
                        maximum(0, g, a)
                if q < QUADS - 1:
                    m_remainder(0, q)
            walk(dve, item)
            normalise(ITEMS - 1, 2)
            normalise(ITEMS - 1, 3)
            add_attention(ITEMS - 1)
            statistics(ITEMS - 1)
            add_mlp(ITEMS - 1)

        @block.gpsimd
        def _(pool):
            G = nc.gpsimd

            def third_part(ip, which):
                pool.wait_ge((q2_done, k2_done)[which], count(ip + 1))
                pool.nop(nofuse=True)
                G.tensor_tensor(parts[:, which, 2, :], rest[:, which, :], parts[:, which, 1, :],
                                ALU.subtract).then_inc((q3_done, k3_done)[which], 1)

            def m_third(im, q):
                pool.wait_ge(m2_done, im * 4 + q + 1)
                pool.nop(nofuse=True)
                G.tensor_tensor(m_parts[:, q % 2, 2, :], m_rest[:, q % 2, :], m_parts[:, q % 2, 1, :],
                                ALU.subtract).then_inc(m3_done, 1)

            def prepare(itt):
                pool.wait_ge(t_loaded, 32 * (itt + 1))
                pool.nop(nofuse=True)
                G.tensor_scalar(omd[:], wt[:, DW0:DW0 + 1], -1.0, 1.0, ALU.mult, ALU.add).then_inc(omd_done, 1)
                G.tensor_scalar(ndw[:], wt[:, DW0:DW0 + 1], -1.0, None, ALU.mult).then_inc(omd_done, 1)
                pool.wait_ge(omd_done, 2 * (itt + 1))
                pool.nop(nofuse=True)
                G.tensor_scalar(bos[:], wt[:, BO0:BO0 + D], omd[:], None, ALU.mult).then_inc(bos_done, 1)
                pool.wait_ge(bos_done, itt + 1)
                pool.nop(nofuse=True)
                pool.wait_ge(x1_done, itt)
                pool.nop(nofuse=True)
                G.tensor_tensor(xb[:], xt[:], bos[:].unsqueeze(1).to_broadcast([P, QT, D]), ALU.add).then_inc(xb_done, 1)

            def combine(itt):
                pool.wait_ge(oq_taken, 4 * (itt + 1))
                pool.nop(nofuse=True)
                G.tensor_scalar(o_neg[:], o_norm[:, :, 1, :], ndw[:], None, ALU.mult).then_inc(neg_done, 1)
                pool.wait_ge(neg_done, itt + 1)
                pool.nop(nofuse=True)
                pool.wait_ge(ot_ready, itt)
                pool.nop(nofuse=True)
                pool.wait_ge(sq_done, QT * itt)
                pool.nop(nofuse=True)
                G.tensor_tensor(o_tok[:].rearrange("p a (h e) -> p (a h) e", h=HEADS), o_norm[:, :, 0, :], o_neg[:],
                                ALU.add).then_inc(o_done, 1)

            def root_mean(itt):
                pool.wait_ge(sq_done, QT * (itt + 1))
                pool.nop(nofuse=True)
                G.tensor_scalar(rms[:], sumsq[:], 1.0 / D, RMS_EPS, ALU.mult, ALU.add).then_inc(ms_done, 1)
                pool.wait_ge(ms_done, itt + 1)
                pool.nop(nofuse=True)
                G.tensor_tensor(rms[:], rms[:], half[:], ALU.pow).then_inc(pow_done, 1)
                pool.wait_ge(pow_done, itt + 1)
                pool.nop(nofuse=True)
                G.tensor_scalar(rms[:], rms[:], omd[:], None, ALU.mult).then_inc(rms_done, 1)

            def norm_x(itt):
                pool.wait_ge(mv_done, itt + 1)
                pool.nop(nofuse=True)
                G.tensor_scalar(rstd[:], mv[:, :, 1], LN_EPS, None, ALU.add).then_inc(ve_done, 1)
                pool.wait_ge(ve_done, itt + 1)
                pool.nop(nofuse=True)
                G.tensor_tensor(rstd[:], rstd[:], half[:], ALU.pow).then_inc(rs_done, 1)
                pool.wait_ge(rs_done, itt + 1)
                pool.nop(nofuse=True)
                pool.wait_ge(ht_ready, itt)
                pool.nop(nofuse=True)
                for a in range(QT):
                    G.tensor_scalar(xn[:, a, :], x1[:, a, :], mv[:, a, 0:1], rstd[:, a:a + 1],
                                    ALU.subtract, ALU.mult).then_inc(xn_done, 1)
                pool.wait_ge(x2_done, itt)
                pool.nop(nofuse=True)
                G.tensor_tensor(x1b[:], x1[:], wt[:, B20:B20 + D].unsqueeze(1).to_broadcast([P, QT, D]),
                                ALU.add).then_inc(x1b_done, 1)

            def item(it, par, inner=False):
                tail, tail_end, maxima, projections = runs(it, inner)
                if tail:
                    prepare(it - 1)
                    combine(it - 1)
                m_third(it, 3)
                if tail:
                    root_mean(it - 1)
                if maxima:
                    m_third(it + 1, 0)
                if tail:
                    norm_x(it - 1)
                if projections:
                    third_part(it + 2, 0)
                    third_part(it + 2, 1)
                if maxima:
                    m_third(it + 1, 1)
                    m_third(it + 1, 2)

            G.memset(half[:], -0.5).then_inc(half_ready, 1)
            pool.wait_ge(half_ready, 1)
            pool.nop(nofuse=True)
            for ip in range(2):
                third_part(ip, 0)
                third_part(ip, 1)
            for q in range(QUADS - 1):
                m_third(0, q)
            walk(pool, item)
            last = ITEMS - 1
            prepare(last)
            combine(last)
            root_mean(last)
            norm_x(last)
VOCAB = 8000
TAPS = 3
S_KEYS = 250
KT0 = S_KEYS // 2
D_LLM = 1024
LC = D_LLM // P
CROWS0 = COMBOS * E
MROWS0 = CROWS0 + PARTS
SCALE0 = float(E) ** -0.5
GE = 160
OPS3 = 3
NF = 8
ROUND = 12582912.0

WQ0, WOA0, BQ0, BK0 = 0, D, 2 * D, 2 * D + 1
BV0, BOA0 = 2 * D + 2, 3 * D + 2
W2G0 = 4 * D + 2
B2G0 = W2G0 + OPS3 * GE
FIRST0 = B2G0 + OPS3
IOTA0 = FIRST0 + 64
APAR = IOTA0 + 32


def embed_attend_gate(nc, ids, taps, src_t, val_t, w_kv, par_d, w_gate_d, ident_d, x_hist, h_hist,
                      scr_q, scr_k, scr_m):
    with ExitStack() as ctx:
        def sb(name, shape, dt=F32):
            return ctx.enter_context(nc.sbuf_tensor(name, shape, dt))

        def sem(name):
            return ctx.enter_context(nc.semaphore(name))

        ident = sb("t_ident", [P, P])
        par = sb("t_par", [P, APAR])
        w_gate = sb("w_gate", [NF, 2, OPS3 * GE])
        srcT = sb("srcT", [P, LC, S_KEYS])
        valT = sb("valT", [P, LC, S_KEYS])
        wkv = sb("wkv", [P, 2, LC, D])
        idx = sb("idx", [P, TAPS * QT], I32)
        taps_in = sb("taps_in", [P, TAPS, QT, D])
        h0 = sb("h0", [P, QT, D])
        hb = sb("hb", [P, QT, D])
        h1 = sb("h1", [P, QT, D])
        h2 = sb("h2", [P, QT, D])
        x_bd = sb("x_bd", [P, QT, D])
        y_tok = sb("y_tok", [P, QT, D])
        x_out = sb("x_out", [P, QT, D])
        yT = sb("yT", [P, TOK])
        stats = sb("t_stats", [P, QT, 6])
        mv = sb("t_mv", [P, QT, 2])
        rstd = sb("t_rstd", [P, QT])
        half = sb("t_half", [P, QT])
        qf = sb("qf", [P, TOK])
        q_parts = sb("q_parts", [P, PARTS, TOK], BF16)
        q_rest = sb("q_rest", [P, TOK])
        kf = sb("kf", [P, S_KEYS])
        k_parts = sb("k_parts", [P, PARTS, S_KEYS], BF16)
        k_rest = sb("k_rest", [P, S_KEYS])
        q_ops = sb("t_q_ops", [P, HEADS, TOK], BF16)
        k_ops = sb("t_k_ops", [P, HEADS, S_KEYS], BF16)
        v_ops = sb("t_v_ops", [P, 2, HEADS, VW])
        mx = sb("t_mx", [P, HEADS * QT])
        m_parts = sb("t_m_parts", [32, PARTS, P], BF16)
        m_rest = sb("t_m_rest", [32, P])
        probs = sb("t_probs", [P, 2, 4, TOK])
        oT_raw = sb("t_oT_raw", [P, 2, TOK])
        rz = sb("t_rz", [P, 2, QT, 4])
        o_tok = sb("t_o_tok", [P, QT, D])
        oT = sb("t_oT", [P, TOK])
        bits = sb("bits", [P, QT, 64])
        first = sb("first", [P, QT * 4])
        left = sb("left", [P, QT * 4])
        feat = sb("feat", [P, QT, NF])
        fT = sb("fT", [NF, TOK])
        gated = sb("gated", [P, 2, OPS3 * GE])
        y = sb("gate_y", [P, QT, 2, OPS3])
        ysel = sb("ysel", [P, QT, 2, OPS3])
        on = sb("on", [P, QT, 3])
        off = sb("off", [P, QT, 3])
        pick = sb("pick", [P, QT, 3])
        any_on = sb("any_on", [P, QT])
        mark = sb("mark", [P, QT])
        res = sb("res", [P, QT, 2])
        hot = sb("hot", [P, QT, 2, 16])

        s_ps = [ctx.enter_context(nc.psum_tensor(f"t_s_ps{i}", [P, TOK], F32)) for i in range(2)]
        st_ps = [ctx.enter_context(nc.psum_tensor(f"t_st_ps{i}", [P, TOK], F32)) for i in range(2)]
        o_ps = [ctx.enter_context(nc.psum_tensor(f"t_o_ps{i}", [P, TOK], F32)) for i in range(2)]
        work = ctx.enter_context(nc.psum_tensor("t_work", [P, TOK], F32))
        work3 = work[:, :].rearrange("p (a b) -> p a b", a=QT)

        (loaded, gathered, idx_loaded, h0_done, k_ready, v_ready, kv_done, kparts_done, k_stored, k_loaded,
         ones_done, half_done, mv_done, rstd_done, norm_done, turned, turn_taken, q_ready, q_first, q_rest_done,
         q_second, q_third, q_stored, q_loaded, s_ready, s_taken, mxt_ready, m_first, m_rest_done, m_second,
         m_third, m_stored, m_loaded, st_ready, exp_done, pv_done, o_copied, oq_ready, oq_taken, wo_ready,
         hb_done, h1_done, feat_done, hid_ready, hid_taken, h2_done, h_stored, x_done,
         x_stored, dve_step, pool_step, act_step) = [sem("t_" + n) for n in (
             "loaded gathered idx_loaded h0_done k_ready v_ready kv_done kparts_done k_stored k_loaded "
             "ones_done half_done mv_done rstd_done norm_done turned turn_taken q_ready q_first q_rest_done "
             "q_second q_third q_stored q_loaded s_ready s_taken mxt_ready m_first m_rest_done m_second "
             "m_third m_stored m_loaded st_ready exp_done pv_done o_copied oq_ready oq_taken wo_ready "
             "hb_done h1_done feat_done hid_ready hid_taken h2_done h_stored x_done "
             "x_stored dve_step pool_step act_step").split()]
        block = ctx.enter_context(nc.Block())
        LOADS = 7

        @block.sync
        def _(sp):
            for dst, src in ((idx[:], ids[0]), (ident[:], ident_d), (par[:], par_d), (w_gate[:], w_gate_d),
                             (srcT[:], src_t), (valT[:], val_t), (wkv[:], w_kv)):
                sp.dma_start(dst, src).then_inc(idx_loaded if dst.tensor is idx[:].tensor else loaded, 16)
            sp.wait_ge(kparts_done, 1)
            sp.nop(nofuse=True)
            for c in range(COMBOS):
                sp.dma_start(scr_k[c], k_parts[:, K_PART[c], :]).then_inc(k_stored, 16)
            sp.wait_ge(k_stored, 16 * COMBOS)
            sp.nop(nofuse=True)
            sp.wait_ge(ones_done, 2)
            sp.nop(nofuse=True)
            sp.dma_start(k_ops[0:CROWS0], scr_k.rearrange("c (e h) t -> (c e) h t", h=HEADS)).then_inc(k_loaded, 16)

            def sequence(s, more=True):
                if more:
                    sp.wait_ge(gathered, 16 * TAPS * QT * (s + 1))
                    sp.nop(nofuse=True)
                    sp.dma_start(idx[:], ids[s + 1]).then_inc(idx_loaded, 16)
                sp.wait_ge(q_third, s + 1)
                sp.nop(nofuse=True)
                for c in range(COMBOS):
                    sp.dma_start(scr_q[c], q_parts[:, Q_PART[c], :]).then_inc(q_stored, 16)
                sp.wait_ge(q_stored, 16 * COMBOS * (s + 1))
                sp.nop(nofuse=True)
                sp.wait_ge(st_ready, 16 * s)
                sp.nop(nofuse=True)
                sp.dma_start(q_ops[0:CROWS0], scr_q.rearrange("c (e h) t -> (c e) h t", h=HEADS)).then_inc(q_loaded, 16)
                sp.wait_ge(m_third, s + 1)
                sp.nop(nofuse=True)
                sp.dma_start(scr_m.rearrange("c p t -> p c t"), m_parts[:]).then_inc(m_stored, 16)
                sp.wait_ge(m_stored, 16 * (s + 1))
                sp.nop(nofuse=True)
                sp.dma_start(q_ops[CROWS0:MROWS0], scr_m.rearrange("c (h a) t -> c h (a t)", h=HEADS)).then_inc(m_loaded, 16)
                sp.wait_ge(h2_done, s + 1)
                sp.nop(nofuse=True)
                sp.dma_start(h_hist[s], h2[:].rearrange("p a b -> p (a b)")).then_inc(h_stored, 16)
                sp.wait_ge(x_done, s + 1)
                sp.nop(nofuse=True)
                sp.dma_start(x_hist[s], x_out[:].rearrange("p a b -> p (a b)")).then_inc(x_stored, 16)

            sequence(0)
            with sp.Fori(1, SEQS - 1) as s:
                sequence(s)
            sequence(SEQS - 1, more=False)
            sp.wait_ge(h_stored, 16 * SEQS)
            sp.nop(nofuse=True)
            sp.wait_ge(x_stored, 16 * SEQS)
            sp.nop(nofuse=True)

        @block.tensor
        def _(pe):
            mm, tr = nc.tensor.matmul, nc.tensor.transpose
            pe.wait_ge(loaded, 16 * (LOADS - 1))
            for c in range(LC):
                last = mm(work[:, 0:S_KEYS], wkv[:, 0, c, :], srcT[:, c, :], start=c == 0, stop=c == LC - 1)
            last.then_inc(k_ready, 1)
            for kt in range(2):
                for c in range(LC):
                    last = mm(s_ps[kt][0:KT0, 0:D], valT[:, c, kt * KT0:(kt + 1) * KT0], wkv[:, 1, c, :],
                              start=c == 0, stop=c == LC - 1)
            last.then_inc(v_ready, 1)
            pe.wait_ge(kv_done, 3)
            pe.wait_ge(k_loaded, 16)

            def turn(src, wanted, value, n=P):
                pe.wait_ge(wanted, count(value))
                for a in range(QT):
                    last = tr(work[0:n, a * P:(a + 1) * P], src[:, a, :], ident[:])
                last.then_inc(turned, 1)

            def sequence(s):
                turn(y_tok, norm_done, s + 1)
                pe.wait_ge(turn_taken, 3 * s + 1)
                mm(work[:], par[:, WQ0:WQ0 + D], yT[:], start=True, stop=True).then_inc(q_ready, 1)
                pe.wait_ge(q_loaded, 16 * (s + 1))
                for t in range(HEADS // 2 * QT):
                    hp, a = t // QT, t % QT
                    if t > 0:
                        pe.wait_ge(s_taken, count(s * 16 + t - 1))
                    for i in range(2):
                        h = 2 * hp + i
                        last = mm(s_ps[t % 2][:, i * S_KEYS:(i + 1) * S_KEYS], q_ops[0:CROWS0, h, a * P:(a + 1) * P],
                                  k_ops[0:CROWS0, h, :], start=True, stop=True)
                    last.then_inc(s_ready, 1)
                pe.wait_ge(s_taken, (s + 1) * 16)
                tr(work[0:HEADS * QT, 0:P], mx[:], ident[:]).then_inc(mxt_ready, 1)
                pe.wait_ge(m_loaded, 16 * (s + 1))

                def weigh(n):
                    q, kt = n // 2, n % 2
                    pe.wait_ge(exp_done, s * 16 + 4 * n + 4)
                    if kt == 0:
                        pe.wait_ge(o_copied, 2 * s)
                    for j in range(4):
                        last = mm(o_ps[q][32 * j:32 * j + VW, :], v_ops[0:KT0, kt, 4 * q + j, :],
                                  probs[0:KT0, n % 2, j, :], start=kt == 0, stop=kt == 1)
                    last.then_inc(pv_done, 1)

                for n in range(4):
                    q, kt = n // 2, n % 2
                    for j in range(4):
                        h = 4 * q + j
                        if n or j:
                            pe.wait_ge(exp_done, count(s * 16 + 4 * n + j - 1))
                        mm(st_ps[j % 2][0:KT0, :], k_ops[0:MROWS0, h, kt * KT0:(kt + 1) * KT0], q_ops[0:MROWS0, h, :],
                           start=True, stop=True).then_inc(st_ready, 1)
                    if n > 0:
                        weigh(n - 1)
                weigh(3)
                for q in range(2):
                    pe.wait_ge(o_copied, 2 * s + q + 1)
                    pe.wait_ge(oq_taken, 2 * s + q)
                    for a in range(QT):
                        last = tr(work3[:, a, :], oT_raw[:, q, a * P:(a + 1) * P], ident[:])
                    last.then_inc(oq_ready, 1)
                turn(o_tok, oq_taken, 2 * s + 2)
                pe.wait_ge(turn_taken, 3 * s + 2)
                for a in range(QT):
                    last = mm(work3[:, a, :], oT[:, a * P:(a + 1) * P], par[:, WOA0:WOA0 + D], start=True, stop=True)
                last.then_inc(wo_ready, 1)
                turn(feat, feat_done, s + 1, NF)
                pe.wait_ge(turn_taken, 3 * s + 3)
                for t in range(2 * QT):
                    a, i = t // 2, t % 2
                    if t > 0:
                        pe.wait_ge(hid_taken, count(s * 2 * QT + t - 1))
                    mm(s_ps[i][:, 0:OPS3 * GE], fT[:, a * P:(a + 1) * P], w_gate[:, i, :],
                       start=True, stop=True).then_inc(hid_ready, 1)
                pe.wait_ge(hid_taken, (s + 1) * 2 * QT)

            sequence(0)
            with pe.Fori(1, SEQS) as s:
                sequence(s)

        @block.scalar
        def _(act):
            A, copy = nc.scalar.activation, nc.scalar.copy
            act.wait_ge(loaded, 16 * (LOADS - 1))
            act.wait_ge(k_ready, 1)
            A(kf[:], work[:, 0:S_KEYS], ACT.Identity, bias=par[:, BK0:BK0 + 1]).then_inc(kv_done, 1)

            def sequence(s):
                act.wait_ge(turned, 3 * s + 1)
                copy(yT[:], work[:]).then_inc(turn_taken, 1)
                act.wait_ge(q_ready, s + 1)
                A(qf[:], work[:], ACT.Identity, bias=par[:, BQ0:BQ0 + 1]).then_inc(act_step, 1)
                act.wait_ge(act_step, s + 1)
                act.wait_ge(q_stored, 16 * COMBOS * s)
                copy(q_parts[:, 0, :], qf[:]).then_inc(q_first, 1)
                act.wait_ge(q_rest_done, s + 1)
                copy(q_parts[:, 1, :], q_rest[:]).then_inc(q_second, 1)
                act.wait_ge(mxt_ready, s + 1)
                act.wait_ge(m_stored, 16 * s)
                A(m_parts[:, 0, :], work[0:32, 0:P], ACT.Copy, scale=-1.0).then_inc(m_first, 1)
                act.wait_ge(m_rest_done, s + 1)
                copy(m_parts[:, 1, :], m_rest[:]).then_inc(m_second, 1)
                for n in range(4):
                    if n > 0:
                        act.wait_ge(pv_done, count(4 * s + n - 1))
                    for j in range(4):
                        act.wait_ge(st_ready, s * 16 + 4 * n + j + 1)
                        A(probs[0:KT0, n % 2, j, :], st_ps[j % 2][0:KT0, :], ACT.Exp, scale=SCALE0).then_inc(exp_done, 1)
                for q in range(2):
                    act.wait_ge(pv_done, 4 * s + 2 * q + 2)
                    copy(oT_raw[:, q, :], o_ps[q][:]).then_inc(o_copied, 1)
                act.wait_ge(turned, 3 * s + 2)
                copy(oT[:], work[:]).then_inc(turn_taken, 1)
                act.wait_ge(turned, 3 * s + 3)
                copy(fT[:], work[0:NF, :]).then_inc(turn_taken, 1)

            sequence(0)
            with act.Fori(1, SEQS) as s:
                sequence(s)

        @block.vector
        def _(dve):
            V = nc.vector
            stepped = [0]
            PER = 46

            def step(ins, s):
                stepped[0] += 1
                ins.then_inc(dve_step, 1)
                dve.wait_ge(dve_step, s * PER + stepped[0])
                dve.nop(nofuse=True)

            V.memset(k_ops[96:128, :, :], 1.0).then_inc(ones_done, 1)
            V.memset(feat[:, :, NF - 1:NF], 1.0).then_inc(ones_done, 1)
            V.memset(v_ops[:], 0.0).then_inc(ones_done, 1)
            dve.wait_ge(ones_done, 3)
            V.memset(v_ops[:, :, :, E:E + 1], 1.0).then_inc(ones_done, 1)
            dve.wait_ge(ones_done, 4)
            dve.wait_ge(loaded, 16 * (LOADS - 1))
            dve.wait_ge(v_ready, 1)
            for kt in range(2):
                V.tensor_tensor(v_ops[0:KT0, kt, :, 0:E], s_ps[kt][0:KT0, 0:D].rearrange("p (h e) -> p h e", h=HEADS),
                                par[0:KT0, BV0:BV0 + D].rearrange("p (h e) -> p h e", h=HEADS), ALU.add).then_inc(kv_done, 1)
            dve.wait_ge(kv_done, 3)
            V.tensor_copy(k_parts[:, 0, :], kf[:]).then_inc(half_done, 1)
            dve.wait_ge(half_done, 2)
            V.tensor_tensor(k_rest[:], kf[:], k_parts[:, 0, :], ALU.subtract).then_inc(half_done, 1)
            dve.wait_ge(half_done, 3)
            V.tensor_copy(k_parts[:, 1, :], k_rest[:]).then_inc(half_done, 1)
            dve.wait_ge(half_done, 4)
            V.tensor_tensor(k_parts[:, 2, :], k_rest[:], k_parts[:, 1, :], ALU.subtract).then_inc(kparts_done, 1)

            def statistics(x, s):
                for a in range(QT):
                    last = V.bn_stats(stats[:, a, :], x[:, a, :])
                step(last, s)
                for a in range(QT):
                    last = V.bn_aggr(mv[:, a, :], stats[:, a, :])
                last.then_inc(mv_done, 1)

            def normalise(out, x, n):
                dve.wait_ge(rstd_done, n)
                for a in range(QT):
                    last = V.tensor_scalar(out[:, a, :], x[:, a, :], mv[:, a, 0:1], rstd[:, a:a + 1],
                                           ALU.subtract, ALU.mult)
                return last

            def sequence(s):
                stepped[0] = 0
                dve.wait_ge(gathered, 16 * TAPS * QT * (s + 1))
                step(V.tensor_tensor(h0[:], taps_in[:, 0], taps_in[:, 1], ALU.add), s)
                V.tensor_tensor(h0[:], h0[:], taps_in[:, 2], ALU.add).then_inc(h0_done, 1)
                dve.wait_ge(h0_done, s + 1)
                statistics(h0, s)
                normalise(y_tok, h0, 3 * s + 1).then_inc(norm_done, 1)
                dve.wait_ge(q_first, s + 1)
                V.tensor_tensor(q_rest[:], qf[:], q_parts[:, 0, :], ALU.subtract).then_inc(q_rest_done, 1)
                for t in range(HEADS // 2 * QT):
                    hp, a = t // QT, t % QT
                    dve.wait_ge(s_ready, s * 16 + t + 1)
                    V.reduce_max(mx[:].rearrange("p (h a) -> p h a", a=QT)[:, 2 * hp:2 * hp + 2, a],
                                 s_ps[t % 2][:, 0:2 * S_KEYS].rearrange("p (i t) -> p i t", i=2), AX.X).then_inc(s_taken, 1)
                dve.wait_ge(m_first, s + 1)
                V.scalar_tensor_tensor(out=m_rest[:], in0=work[0:32, 0:P], scalar=-1.0, in1=m_parts[:, 0, :],
                                       op0=ALU.mult, op1=ALU.subtract).then_inc(m_rest_done, 1)
                for q in range(2):
                    src = work[:].rearrange("p (a j w) -> p a j w", a=QT, j=4)
                    dve.wait_ge(oq_ready, 2 * s + q + 1)
                    step(V.reciprocal(rz[:, q, :, :], src[:, :, :, E]), s)
                    V.tensor_tensor(o_tok[:].rearrange("p a (q j e) -> p a q j e", q=2, j=4)[:, :, q], src[:, :, :, 0:E],
                                    rz[:, q, :, :].unsqueeze(3).to_broadcast([P, QT, 4, E]), ALU.mult).then_inc(oq_taken, 1)
                dve.wait_ge(wo_ready, s + 1)
                dve.wait_ge(hb_done, s + 1)
                V.tensor_tensor(h1[:], work3[:], hb[:], ALU.add).then_inc(h1_done, 1)
                dve.wait_ge(h1_done, s + 1)
                statistics(h1, s)
                step(normalise(x_bd, h1, 3 * s + 2), s)
                step(V.scalar_tensor_tensor(out=bits[:], in0=x_bd[:, :, 16:80], scalar=0.5,
                                            in1=par[:, FIRST0:FIRST0 + 64].unsqueeze(1).to_broadcast([P, QT, 64]),
                                            op0=ALU.is_gt, op1=ALU.mult), s)
                step(V.reduce_max(first[:], bits[:].rearrange("p a (n j) -> p (a n) j", j=16), AX.X), s)
                step(V.tensor_scalar(left[:], first[:], -1.0, 16.0, ALU.mult, ALU.add), s)
                step(V.scalar_tensor_tensor(out=feat[:, :, 0:4], in0=first[:].rearrange("p (a n) -> p a n", a=QT),
                                            scalar=0.0, in1=left[:].rearrange("p (a n) -> p a n", a=QT),
                                            op0=ALU.is_gt, op1=ALU.mult), s)
                V.tensor_copy(feat[:, :, 4:7], x_bd[:, :, 1:4]).then_inc(feat_done, 1)
                step(V.tensor_single_scalar(on[:], x_bd[:, :, 1:4], 0.5, ALU.is_gt), s)
                step(V.tensor_scalar(off[:], on[:], -1.0, 1.0, ALU.mult, ALU.add), s)
                step(V.tensor_copy(pick[:, :, 0:1], on[:, :, 0:1]), s)
                step(V.tensor_tensor(pick[:, :, 1:2], on[:, :, 1:2], off[:, :, 0:1], ALU.mult), s)
                step(V.tensor_tensor(pick[:, :, 2:3], off[:, :, 1:2], off[:, :, 0:1], ALU.mult), s)
                step(V.reduce_max(any_on[:], on[:], AX.X), s)
                step(V.tensor_scalar(mark[:], x_bd[:, :, 0], 0.5, 2.0, ALU.is_ge, ALU.mult), s)
                step(V.tensor_tensor(mark[:], mark[:], any_on[:], ALU.mult), s)
                for t in range(2 * QT):
                    a, i = t // 2, t % 2
                    dve.wait_ge(hid_ready, s * 2 * QT + t + 1)
                    for o in range(OPS3):
                        last = V.scalar_tensor_tensor(out=gated[:, i, o * GE:(o + 1) * GE], in0=s_ps[i][:, o * GE:(o + 1) * GE],
                                                      scalar=0.0, in1=par[:, W2G0 + o * GE:W2G0 + (o + 1) * GE],
                                                      op0=ALU.max, op1=ALU.mult, accum_out=y[:, a, i, o:o + 1])
                    last.then_inc(hid_taken, 1)
                dve.wait_ge(hid_taken, (s + 1) * 2 * QT)
                step(V.tensor_tensor(y[:].rearrange("p a i o -> p (a i) o"), y[:].rearrange("p a i o -> p (a i) o"),
                                     par[:, B2G0:B2G0 + OPS3].unsqueeze(1).to_broadcast([P, 2 * QT, OPS3]), ALU.add), s)
                step(V.tensor_tensor(ysel[:], y[:], pick[:].unsqueeze(2).to_broadcast([P, QT, 2, OPS3]), ALU.mult), s)
                step(V.reduce_sum(res[:], ysel[:], AX.X), s)
                step(V.tensor_scalar(res[:], res[:], 0.0, 15.0, ALU.max, ALU.min), s)
                step(V.tensor_scalar(res[:], res[:], ROUND, ROUND, ALU.add, ALU.subtract), s)
                step(V.tensor_tensor(hot[:], par[:, IOTA0:IOTA0 + 32].rearrange("p (i j) -> p i j", i=2).unsqueeze(1)
                                     .to_broadcast([P, QT, 2, 16]), res[:].unsqueeze(3).to_broadcast([P, QT, 2, 16]),
                                     ALU.is_equal), s)
                step(V.tensor_tensor(hot[:].rearrange("p a i j -> p a (i j)"), hot[:].rearrange("p a i j -> p a (i j)"),
                                     mark[:].unsqueeze(2).to_broadcast([P, QT, 32]), ALU.mult), s)
                step(V.tensor_tensor(x_bd[:, :, 80:112], x_bd[:, :, 80:112], hot[:].rearrange("p a i j -> p a (i j)"),
                                     ALU.add), s)
                dve.wait_ge(h_stored, 16 * s)
                V.tensor_tensor(h2[:], h1[:], x_bd[:], ALU.add).then_inc(h2_done, 1)
                dve.wait_ge(h2_done, s + 1)
                statistics(h2, s)
                dve.wait_ge(x_stored, 16 * s)
                normalise(x_out, h2, 3 * s + 3).then_inc(x_done, 1)
                while stepped[0] < PER:
                    step(V.tensor_copy(any_on[:], mark[:]), s)

            sequence(0)
            with dve.Fori(1, SEQS) as s:
                sequence(s)

        @block.gpsimd
        def _(pool):
            G = nc.gpsimd
            G.memset(half[:], -0.5).then_inc(half_done, 1)

            def gather(s):
                pool.wait_ge(idx_loaded, 16 * (s + 1))
                pool.nop(nofuse=True)
                pool.wait_ge(h0_done, s)
                pool.nop(nofuse=True)
                for k in range(TAPS):
                    for a in range(QT):
                        c = k * QT + a
                        G.indirect_dma_start(taps_in[:, k, a, :], None, taps[k],
                                             bass.IndirectOffsetOnAxis(ap=idx[:, c:c + 1], axis=0)).then_inc(gathered, 16)

            def root(n):
                pool.wait_ge(mv_done, n)
                pool.nop(nofuse=True)
                G.tensor_scalar(rstd[:], mv[:, :, 1], LN_EPS, None, ALU.add).then_inc(pool_step, 1)
                pool.wait_ge(pool_step, n)
                pool.nop(nofuse=True)
                G.tensor_tensor(rstd[:], rstd[:], half[:], ALU.pow).then_inc(rstd_done, 1)

            def sequence(s, more=True):
                root(3 * s + 1)
                if more:
                    gather(s + 1)
                pool.wait_ge(q_second, s + 1)
                pool.nop(nofuse=True)
                G.tensor_tensor(q_parts[:, 2, :], q_rest[:], q_parts[:, 1, :], ALU.subtract).then_inc(q_third, 1)
                pool.wait_ge(h0_done, s + 1)
                pool.nop(nofuse=True)
                G.tensor_tensor(hb[:], h0[:], par[:, BOA0:BOA0 + D].unsqueeze(1).to_broadcast([P, QT, D]),
                                ALU.add).then_inc(hb_done, 1)
                pool.wait_ge(m_second, s + 1)
                pool.nop(nofuse=True)
                G.tensor_tensor(m_parts[:, 2, :], m_rest[:], m_parts[:, 1, :], ALU.subtract).then_inc(m_third, 1)
                root(3 * s + 2)
                root(3 * s + 3)

            gather(0)
            pool.wait_ge(loaded, 16 * (LOADS - 1))
            pool.nop(nofuse=True)
            sequence(0)
            with pool.Fori(1, SEQS - 1) as s:
                sequence(s)
            sequence(SEQS - 1, more=False)


WL0, BL0, GF0, BF0 = 0, D, 2 * D, 3 * D
LPAR = 4 * D


def quantised_layer(nc, par_d, ident_d, x_hist, h_hist, out):
    with ExitStack() as ctx:
        def sb(name, shape, dt=F32):
            return ctx.enter_context(nc.sbuf_tensor(name, shape, dt))

        def sem(name):
            return ctx.enter_context(nc.semaphore(name))

        ident = sb("f_ident", [P, P])
        par = sb("f_par", [P, LPAR])
        ones = sb("f_ones", [P, P])
        sums = sb("f_sums", [P, 2])
        means = sb("f_means", [P, 2])
        wc = sb("f_wc", [P, D])
        pos = sb("f_pos", [P, D])
        neg = sb("f_neg", [P, D])
        w_eff = sb("w_eff", [P, D])
        B = 2
        xf = [sb(f"f_xf{i}", [P, QT, D]) for i in range(B)]
        hh = [sb(f"f_hh{i}", [P, QT, D]) for i in range(B)]
        xg = [sb(f"f_xg{i}", [P, QT, D]) for i in range(B)]
        h3 = [sb(f"f_h3{i}", [P, QT, D]) for i in range(B)]
        yn = [sb(f"f_yn{i}", [P, QT, D]) for i in range(B)]
        yT = [sb(f"f_yT{i}", [P, TOK]) for i in range(B)]
        yb = [sb(f"f_yb{i}", [P, QT, D]) for i in range(B)]
        rq = [sb(f"f_rq{i}", [P, QT, D]) for i in range(B)]
        fin = [sb(f"f_fin{i}", [P, QT, D]) for i in range(B)]
        stats = [sb(f"f_stats{i}", [P, QT, 6]) for i in range(2 * B)]
        mv = [sb(f"f_mv{i}", [P, QT, 2]) for i in range(2 * B)]
        rstd = [sb(f"f_rstd{i}", [P, QT]) for i in range(2 * B)]
        half = sb("f_half", [P, QT])
        turn_ps = [ctx.enter_context(nc.psum_tensor(f"f_turn{i}", [P, TOK], F32)) for i in range(2)]
        y_ps = [ctx.enter_context(nc.psum_tensor(f"f_y{i}", [P, TOK], F32)) for i in range(2)]
        (loaded, x_loaded, h_loaded, ones_done, sums_done, sums_ready, means_done, w_step, w_done, half_done, stats_done,
         mv_done, ve_done, rstd_done, xg_done, h3_done, yn_done, turned, yT_done, y_ready, step_done, fin_done,
         stored, gx_done) = [sem("f_" + n) for n in (
             "loaded x_loaded h_loaded ones_done sums_done sums_ready means_done w_step w_done half_done stats_done "
             "mv_done ve_done rstd_done xg_done h3_done yn_done turned yT_done y_ready step_done fin_done "
             "stored gx_done").split()]
        block = ctx.enter_context(nc.Block())

        def pairs(eng, sequence):
            sequence(0, 0)
            sequence(1, 1)
            with eng.Fori(1, SEQS // 2) as pair:
                for b in range(2):
                    sequence(pair * 2 + b, b)

        @block.sync
        def _(sp):
            sp.dma_start(ident[:], ident_d).then_inc(loaded, 16)
            sp.dma_start(par[:], par_d).then_inc(loaded, 16)

            def sequence(s, b):
                sp.wait_ge(h3_done, count(s - 1))
                sp.nop(nofuse=True)
                sp.wait_ge(h_loaded, 32 * s)
                sp.nop(nofuse=True)
                sp.dma_start(xf[b][:], x_hist[LAYERS * SEQS + s].rearrange("p (a b) -> p a b", a=QT)).then_inc(h_loaded, 16)
                sp.dma_start(hh[b][:], h_hist[s].rearrange("p (a b) -> p a b", a=QT)).then_inc(h_loaded, 16)

            sequence(0, 0)

            def both(s, b, more=True):
                if more:
                    sequence(s + 1, 1 - b)
                sp.wait_ge(fin_done, s + 1)
                sp.nop(nofuse=True)
                sp.dma_start(out[s].rearrange("(a p) d -> p a d", p=P), fin[b][:]).then_inc(stored, 16)
                sp.wait_ge(stored, 16 * (s + 1))
                sp.nop(nofuse=True)

            both(0, 0)
            both(1, 1)
            with sp.Fori(1, SEQS // 2 - 1) as pair:
                for b in range(2):
                    both(pair * 2 + b, b)
            both(SEQS - 2, 0)
            both(SEQS - 1, 1, more=False)

        @block.tensor
        def _(pe):
            mm, tr = nc.tensor.matmul, nc.tensor.transpose
            pe.wait_ge(ones_done, 1)
            pe.wait_ge(sums_done, 3)
            mm(y_ps[0][:, 0:2], ones[:], sums[:], start=True, stop=True).then_inc(sums_ready, 1)
            pe.wait_ge(w_done, 1)

            def sequence(s, b):
                pe.wait_ge(yn_done, s + 1)
                pe.wait_ge(yT_done, count(s - 1))
                for a in range(QT):
                    last = tr(turn_ps[b][:, a * P:(a + 1) * P], yn[b][:, a, :], ident[:])
                last.then_inc(turned, 1)
                pe.wait_ge(yT_done, s + 1)
                pe.wait_ge(fin_done, count(s - 1))
                for a in range(QT):
                    last = mm(y_ps[b][:, a * P:(a + 1) * P], yT[b][:, a * P:(a + 1) * P], w_eff[:], start=True, stop=True)
                last.then_inc(y_ready, 1)

            pairs(pe, sequence)

        @block.scalar
        def _(act):
            def sequence(s, b):
                act.wait_ge(turned, s + 1)
                act.wait_ge(y_ready, count(s - 1))
                nc.scalar.copy(yT[b][:], turn_ps[b][:]).then_inc(yT_done, 1)

            pairs(act, sequence)

        @block.vector
        def _(dve):
            V = nc.vector
            w = par[:, WL0:WL0 + D]
            dve.wait_ge(loaded, 32)
            n = [0]

            def w_link(ins):
                n[0] += 1
                ins.then_inc(w_step, 1)
                dve.wait_ge(w_step, n[0])

            V.memset(ones[:], 1.0).then_inc(ones_done, 1)
            V.reduce_sum(sums[:, 0:1], w, AX.X).then_inc(sums_done, 1)
            V.scalar_tensor_tensor(out=wc[:], in0=w, scalar=-1.0, in1=w, op0=ALU.mult, op1=ALU.max).then_inc(sums_done, 1)
            dve.wait_ge(sums_done, 2)
            V.reduce_sum(sums[:, 1:2], wc[:], AX.X).then_inc(sums_done, 1)
            dve.wait_ge(sums_ready, 1)
            w_link(V.tensor_scalar(means[:], y_ps[0][:, 0:2], 1.0 / (D * D), None, ALU.mult))
            w_link(V.tensor_scalar(wc[:], w, means[:, 0:1], None, ALU.subtract))
            w_link(V.tensor_single_scalar(pos[:], wc[:], 0.0, ALU.is_gt))
            w_link(V.tensor_single_scalar(neg[:], wc[:], 0.0, ALU.is_lt))
            w_link(V.tensor_tensor(pos[:], pos[:], neg[:], ALU.subtract))
            w_link(V.tensor_tensor(pos[:], pos[:], w, ALU.subtract))
            w_link(V.tensor_tensor(pos[:], pos[:], w, ALU.add))
            V.tensor_scalar(w_eff[:], pos[:], means[:, 1:2], None, ALU.mult).then_inc(w_done, 1)

            def statistics(x, i, k):
                for a in range(QT):
                    last = V.bn_stats(stats[i][:, a, :], x[:, a, :])
                last.then_inc(stats_done, 1)
                dve.wait_ge(stats_done, k)
                dve.nop(nofuse=True)
                for a in range(QT):
                    last = V.bn_aggr(mv[i][:, a, :], stats[i][:, a, :])
                last.then_inc(mv_done, 1)

            def sequence(s, b):
                dve.wait_ge(h_loaded, 32 * (s + 1))
                statistics(xf[b], b, 2 * s + 1)
                dve.wait_ge(xg_done, s + 1)
                V.tensor_tensor(h3[b][:], xg[b][:], hh[b][:], ALU.add).then_inc(h3_done, 1)
                dve.wait_ge(h3_done, s + 1)
                statistics(h3[b], 2 + b, 2 * s + 2)
                dve.wait_ge(y_ready, s + 1)
                steps = (
                    lambda: V.tensor_tensor(yb[b][:], y_ps[b][:].rearrange("p (a d) -> p a d", a=QT),
                                            par[:, BL0:BL0 + D].unsqueeze(1).to_broadcast([P, QT, D]), ALU.add),
                    lambda: V.tensor_scalar(rq[b][:], yb[b][:], -1.0, 1.0, ALU.max, ALU.min),
                    lambda: V.tensor_scalar(rq[b][:], rq[b][:], 7.0, ROUND, ALU.mult, ALU.add),
                    lambda: V.tensor_scalar(rq[b][:], rq[b][:], ROUND, 1.0 / 7.0, ALU.subtract, ALU.mult),
                    lambda: V.tensor_tensor(rq[b][:], rq[b][:], yb[b][:], ALU.subtract),
                    lambda: V.tensor_tensor(rq[b][:], rq[b][:], yb[b][:], ALU.add),
                )
                for k, f in enumerate(steps):
                    f().then_inc(step_done, 1)
                    dve.wait_ge(step_done, len(steps) * s + k + 1)
                dve.wait_ge(stored, count(16 * (s - 1)))
                V.tensor_tensor(fin[b][:], rq[b][:], h3[b][:], ALU.add).then_inc(fin_done, 1)

            pairs(dve, sequence)

        @block.gpsimd
        def _(pool):
            G = nc.gpsimd
            G.memset(half[:], -0.5).then_inc(half_done, 1)
            pool.wait_ge(half_done, 1)
            pool.nop(nofuse=True)
            pool.wait_ge(loaded, 32)
            pool.nop(nofuse=True)

            def root(i, k):
                pool.wait_ge(mv_done, k)
                pool.nop(nofuse=True)
                G.tensor_scalar(rstd[i][:], mv[i][:, :, 1], LN_EPS, None, ALU.add).then_inc(ve_done, 1)
                pool.wait_ge(ve_done, k)
                pool.nop(nofuse=True)
                G.tensor_tensor(rstd[i][:], rstd[i][:], half[:], ALU.pow).then_inc(rstd_done, 1)
                pool.wait_ge(rstd_done, k)
                pool.nop(nofuse=True)

            def normalise(out_t, x, i, done):
                for a in range(QT):
                    last = G.tensor_scalar(out_t[:, a, :], x[:, a, :], mv[i][:, a, 0:1], rstd[i][:, a:a + 1],
                                           ALU.subtract, ALU.mult)
                last.then_inc(done, 1)

            def sequence(s, b):
                root(b, 2 * s + 1)
                pool.wait_ge(h3_done, count(s - 1))
                pool.nop(nofuse=True)
                normalise(xg[b], xf[b], b, gx_done)
                pool.wait_ge(gx_done, 2 * s + 1)
                pool.nop(nofuse=True)
                G.tensor_tensor(xg[b][:], xg[b][:], par[:, GF0:GF0 + D].unsqueeze(1).to_broadcast([P, QT, D]),
                                ALU.mult).then_inc(gx_done, 1)
                pool.wait_ge(gx_done, 2 * s + 2)
                pool.nop(nofuse=True)
                G.tensor_tensor(xg[b][:], xg[b][:], par[:, BF0:BF0 + D].unsqueeze(1).to_broadcast([P, QT, D]),
                                ALU.add).then_inc(xg_done, 1)
                root(2 + b, 2 * s + 2)
                pool.wait_ge(turned, count(s - 1))
                pool.nop(nofuse=True)
                normalise(yn[b], h3[b], 2 + b, yn_done)

            pairs(pool, sequence)


def build(nc, a, out):
    def scratch(name, shape, dt=F32):
        return nc.dram_tensor(name, shape, dt).ap()

    x_hist = scratch("x_hist", [(LAYERS + 1) * SEQS, P, QT * D])
    h_hist = scratch("h_hist", [SEQS, P, QT * D])
    embed_attend_gate(nc, a["ids"], (a["tap0"], a["tap1"], a["tap2"]), a["src_t"], a["val_t"], a["w_kv"], a["tower_par"],
                      a["w_gate"], a["ident"], x_hist, h_hist, scratch("t_scr_q", [COMBOS, P, TOK], BF16),
                      scratch("t_scr_k", [COMBOS, P, S_KEYS], BF16), scratch("t_scr_m", [PARTS, HEADS * QT, P], BF16))
    blocks(nc, a["w_qk"], a["w_v"], a["w_tail"], a["ident"], x_hist, scratch("scr_q", [2, COMBOS, P, TOK], BF16),
           scratch("scr_k", [2, COMBOS, P, TOK], BF16), scratch("scr_m", [2, QUADS, PARTS, 16, P], BF16))
    quantised_layer(nc, a["last_par"], a["ident"], x_hist, h_hist, out)


def lay_out(i):
    rows = lambda v: np.broadcast_to(v[None, :], (P, v.shape[0]))
    cols = lambda v: v[:, None]
    a = {}
    padded = np.pad(np.asarray(i["x"]), ((0, 0), (1, 1)), constant_values=VOCAB)
    windows = np.stack([padded[:, k:k + TOK] for k in range(TAPS)], 1)
    a["ids"] = windows.reshape(SEQS, TAPS, QT, P).transpose(0, 3, 1, 2).reshape(SEQS, P, TAPS * QT)
    table = np.pad(i["L0_tok_conv_w"], ((0, 0), (0, 1), (0, 0)))
    for k in range(TAPS):
        a[f"tap{k}"] = table[:, :, k].T
    turn = np.arange(D).reshape(HEADS, E).T.reshape(-1)
    a["src_t"] = i["L0_attn_source_embedding"].reshape(S_KEYS, LC, P).transpose(2, 1, 0)
    a["val_t"] = i["L0_attn_value_embedding"].reshape(S_KEYS, LC, P).transpose(2, 1, 0)
    a["w_kv"] = np.stack([i["L0_attn_Wk"][:, turn].reshape(LC, P, D).transpose(1, 0, 2),
                          i["L0_attn_Wv"].reshape(LC, P, D).transpose(1, 0, 2)], 1)
    ops = ("and", "or", "xor")
    w2 = np.concatenate([i[f"L0_ffn_{o}_w2"][:, 64] for o in ops])
    b2 = np.stack([i[f"L0_ffn_{o}_b2"][64] for o in ops])
    f32 = np.float32
    a["tower_par"] = np.concatenate([
        i["L0_attn_Wq"][:, turn], i["L0_attn_Wo"], cols(i["L0_attn_bq"][turn]), cols(i["L0_attn_bk"][turn]),
        rows(i["L0_attn_bv"]), rows(i["L0_attn_bo"]), rows(w2), rows(b2),
        rows(np.tile(np.arange(16, 0, -1, dtype=f32), 4)), rows(np.tile(np.arange(16, dtype=f32), 2))], 1)
    w1 = np.concatenate([i[f"L0_ffn_{o}_w1"] for o in ops], 1)
    b1 = np.concatenate([i[f"L0_ffn_{o}_b1"] for o in ops])
    none = np.zeros_like(b1)
    a["w_gate"] = np.stack([np.stack([w1[0], none, w1[1], none, w1[46], w1[44], w1[45], b1]),
                            np.stack([none, w1[0], none, w1[1], w1[46], w1[44], w1[45], b1])], 1)
    L = {n: i["L1_attn_" + n] for n in "Wq Wk Wv rms_w Wo bo diffw g_ffn b_ffn W1 b1 W2 b2 g_f b_f".split()}
    turn1 = np.arange(D).reshape(GROUPS, F).T.reshape(-1)
    t = lambda w: w.transpose(0, 2, 1)
    a["w_qk"] = np.stack([t(L["Wq"][:, turn1]), t(L["Wk"][:, turn1])], 2)
    a["w_v"] = t(L["Wv"])
    a["w_tail"] = np.concatenate([
        t(L["Wo"]), t(L["W1"]), t(L["W2"]).reshape(LAYERS, HT, P, D).transpose(0, 2, 1, 3).reshape(LAYERS, P, HID),
        L["rms_w"].reshape(LAYERS, D, 1), L["g_ffn"][:, :, None], L["b_ffn"][:, :, None],
        L["b1"].reshape(LAYERS, HT, P).transpose(0, 2, 1), np.broadcast_to(L["diffw"][:, None, None], (LAYERS, P, 1)),
        np.broadcast_to(L["bo"][:, None, :], (LAYERS, P, D)), np.broadcast_to(L["b2"][:, None, :], (LAYERS, P, D))], 2)
    a["last_par"] = np.concatenate([i["L1_ffn_weight"], rows(i["L1_ffn_bias"]), rows(L["g_f"]), rows(L["b_f"])], 1)
    a["ident"] = np.eye(P, dtype=f32)
    return {n: np.ascontiguousarray(v) for n, v in a.items()}


def kernel(**inputs):
    import concourse.bacc as bacc
    from concourse.bass_utils import run_bass_kernel_spmd

    arrays = lay_out({n: np.asarray(v) for n, v in inputs.items()})
    nc = bacc.Bacc("TRN2", target_bir_lowering=False, num_devices=1)
    nc.disable_value_cache = True
    aps = {n: nc.dram_tensor("in_" + n, v.shape, mybir.dt.from_np(v.dtype), kind="ExternalInput").ap() for n, v in arrays.items()}
    out = nc.dram_tensor("out", (SEQS, TOK, D), F32, kind="ExternalOutput").ap()
    build(nc, aps, out)
    result = run_bass_kernel_spmd(nc, [{"in_" + n: v for n, v in arrays.items()}], core_ids=[0])
    return result.results[0]["out"]
```

```python
from contextlib import ExitStack
import numpy as np
import concourse.bass as bass
from concourse import mybir

F32 = mybir.dt.float32
BF16 = mybir.dt.bfloat16
I32 = mybir.dt.int32
ACT = mybir.ActivationFunctionType
ALU = mybir.AluOpType
AX = mybir.AxisListType

P = 128
D = 128
SEQS = 16
TOK = 512
QT = TOK // P
LAYERS = 4
ITEMS = LAYERS * SEQS

HEADS = 8
GROUPS = 2 * HEADS
F = D // GROUPS
E = D // HEADS
VW = 32
QUADS = GROUPS // 4
STEPS = GROUPS
PARTS = 3
COMBOS = 6
Q_PART = (0, 0, 0, 1, 1, 2)
K_PART = (0, 1, 2, 0, 1, 0)
CROWS = COMBOS * F
MROWS = CROWS + PARTS
SCALE = float(F) ** -0.5
RMS_EPS = 1.1920929e-07
LN_EPS = 1e-05
HID = 512
HT = HID // P

WO0, W10, W20 = 0, D, D + HID
RW0 = D + 2 * HID
G0, B0, B10, DW0, BO0, B20 = RW0 + 1, RW0 + 2, RW0 + 3, RW0 + 3 + HT, RW0 + 4 + HT, RW0 + 4 + HT + D
TPAR = B20 + D


def count(value):
    return max(value, 0) if isinstance(value, int) else value


def blocks(nc, w_qk, w_v, w_tail, ident_d, x_hist, scr_q, scr_k, scr_m):
    with ExitStack() as ctx:
        def sb(name, shape, dt=F32):
            return ctx.enter_context(nc.sbuf_tensor(name, shape, dt))

        def ps(name, shape):
            return ctx.enter_context(nc.psum_tensor(name, shape, F32))

        def sem(name):
            return ctx.enter_context(nc.semaphore(name))

        ident = sb("bl_ident", [P, P])
        q_ops = [sb(f"q_ops{i}", [64, GROUPS, TOK], BF16) for i in range(2)]
        k_ops = [sb(f"k_ops{i}", [64, GROUPS, TOK], BF16) for i in range(2)]
        v_ops = [sb(f"v_ops{i}", [P, QT, HEADS, VW]) for i in range(2)]
        probs = sb("probs", [P, 4, 4, TOK])
        wqk = sb("wqk", [P, 2, D])
        wv = sb("wv", [P, D])
        xs = sb("xs", [P, QT, D])
        xT = sb("xT", [P, TOK])
        parts = sb("parts", [P, 2, PARTS, TOK], BF16)
        rest = sb("rest", [P, 2, TOK])
        mx = sb("mx", [P, 2, 16])
        m_parts = sb("m_parts", [16, 2, PARTS, P], BF16)
        m_rest = sb("m_rest", [16, 2, P])
        oT_raw = sb("oT_raw", [P, 2, TOK])
        rz = sb("rz", [P, 2, QT, 4])
        o_norm = sb("o_norm", [P, QT * HEADS, 2, E])
        o_neg = sb("o_neg", [P, QT * HEADS, E])
        o_tok = sb("o_tok", [P, QT, D])
        junk = sb("junk", [P, QT, D])
        sumsq = sb("sumsq", [P, QT])
        rms = sb("rms", [P, QT])
        half = sb("half", [P, QT])
        omd = sb("omd", [P, 1])
        ndw = sb("ndw", [P, 1])
        bos = sb("bos", [P, D])
        xt = sb("xt", [P, QT, D])
        xb = sb("xb", [P, QT, D])
        x1 = sb("x1", [P, QT, D])
        x1b = sb("x1b", [P, QT, D])
        x2 = sb("x2", [P, QT, D])
        stats = sb("stats", [P, QT, 6])
        mv = sb("mv", [P, QT, 2])
        rstd = sb("rstd", [P, QT])
        xn = sb("xn", [P, QT, D])
        oT = sb("oT", [P, TOK])
        hT = sb("hT", [P, TOK])
        u_in = sb("u_in", [P, HT, TOK])
        u = sb("u", [P, HT, TOK])
        wt = sb("wt", [P, TPAR])

        st_ps = [ps(f"st_ps{i}", [P, TOK]) for i in range(3)]
        s_ps = [ps(f"s_ps{i}", [P, TOK]) for i in range(2)]
        o_ps = ps("o_ps", [P, TOK])
        tail_ps = ps("tail_ps", [P, TOK])
        proj_ps = ps("proj_ps", [P, TOK])
        tail3 = tail_ps[:, :].rearrange("p (a b) -> p a b", a=QT)
        proj3 = proj_ps[:, :].rearrange("p (a b) -> p a b", a=QT)

        names = """const_ready half_ready ident_loaded ones_ready odd_ones_ready
            st_ready exp_done pv_done o_copied oq_ready rz_done oq_taken
            s_ready s_taken mxt_ready m1_done mr_done m2_done m3_done m_written
            wqk_loaded wv_loaded xs_loaded xt_ready xt_done q_ready k_ready q1_done k1_done qr_done kr_done
            q2_done k2_done q3_done k3_done qk_written v_ready v_done
            t_loaded omd_done bos_done xb_done neg_done o_done sq_done ms_done pow_done rms_done
            ot_ready ot_done wo_ready x1_done bn_done mv_done ve_done rs_done xn_done x1b_done ht_ready ht_done
            w1_ready u_in_done gelu_done w2_ready x2_done x_stored""".split()
        S = {n: sem(n) for n in names}
        op_loaded = [sem(f"op_loaded{q}") for q in range(QUADS)]
        m_loaded = [sem(f"m_loaded{q}") for q in range(QUADS)]
        (const_ready, half_ready, ident_loaded, ones_ready, odd_ones_ready,
         st_ready, exp_done, pv_done, o_copied, oq_ready, rz_done, oq_taken,
         s_ready, s_taken, mxt_ready, m1_done, mr_done, m2_done, m3_done, m_written,
         wqk_loaded, wv_loaded, xs_loaded, xt_ready, xt_done, q_ready, k_ready, q1_done, k1_done, qr_done, kr_done,
         q2_done, k2_done, q3_done, k3_done, qk_written, v_ready, v_done,
         t_loaded, omd_done, bos_done, xb_done, neg_done, o_done, sq_done, ms_done, pow_done, rms_done,
         ot_ready, ot_done, wo_ready, x1_done, bn_done, mv_done, ve_done, rs_done, xn_done, x1b_done, ht_ready, ht_done,
         w1_ready, u_in_done, gelu_done, w2_ready, x2_done, x_stored) = [S[n] for n in names]
        block = ctx.enter_context(nc.Block())

        def walk(eng, item):
            for i in range(2):
                item(i, i)
            with eng.Fori(1, ITEMS // 2 - 1) as pair:
                for par in range(2):
                    item(pair * 2 + par, par, inner=True)
            for i in range(ITEMS - 2, ITEMS):
                item(i, i % 2)

        def st_bank(par, s, j):
            return (par * 64 + 4 * s + j) % 3

        def runs(it, inner):
            if inner:
                return True, True, True, True
            return it >= 1, it >= 2, it + 1 < ITEMS, it + 2 < ITEMS

        @block.sync
        def _(sp):
            def load_projection_inputs(ip):
                sp.wait_ge(xt_ready, ip)
                sp.nop(nofuse=True)
                sp.dma_start(xs[:], x_hist[ip].rearrange("p (a b) -> p a b", a=QT)).then_inc(xs_loaded, 16)
                sp.wait_ge(k_ready, ip)
                sp.nop(nofuse=True)
                sp.dma_start(wqk[:], w_qk[ip // SEQS]).then_inc(wqk_loaded, 16)

            def load_value_weights(iv):
                sp.wait_ge(v_ready, iv)
                sp.nop(nofuse=True)
                sp.dma_start(wv[:], w_v[iv // SEQS]).then_inc(wv_loaded, 16)

            def stage_operands(ip, par):
                for q in range(QUADS):
                    sp.wait_ge(op_loaded[q], count(32 * (ip - 1)))
                    sp.nop(nofuse=True)
                for done, which, scr, part in ((q3_done, 0, scr_q, Q_PART), (k3_done, 1, scr_k, K_PART)):
                    sp.wait_ge(done, ip + 1)
                    sp.nop(nofuse=True)
                    for c in range(COMBOS):
                        sp.dma_start(scr[par, c], parts[:, which, part[c], :]).then_inc(qk_written, 16)
                sp.wait_ge(qk_written, 2 * COMBOS * 16 * (ip + 1))
                sp.nop(nofuse=True)

            def load_operands(ip, par, q):
                sp.wait_ge(st_ready, count((ip - 2) * 64 + 16 * (q + 1)))
                sp.nop(nofuse=True)
                for ops, scr in ((q_ops, scr_q), (k_ops, scr_k)):
                    src = scr[par].rearrange("c (d g) t -> (c d) g t", g=GROUPS)[:, 4 * q:4 * q + 4, :]
                    sp.dma_start(ops[par][0:CROWS, 4 * q:4 * q + 4, :], src).then_inc(op_loaded[q], 16)

            def move_maxima(im, par, q):
                sp.wait_ge(m3_done, im * 4 + q + 1)
                sp.nop(nofuse=True)
                sp.dma_start(scr_m[par, q].rearrange("c p t -> p c t"), m_parts[:, q % 2, :, :]).then_inc(m_written, 16)
                sp.wait_ge(m_written, 16 * (im * 4 + q + 1))
                sp.nop(nofuse=True)
                sp.wait_ge(st_ready, count((im - 2) * 64 + 16 * (q + 1)))
                sp.nop(nofuse=True)
                sp.dma_start(q_ops[par][CROWS:MROWS, 4 * q:4 * q + 4, :],
                             scr_m[par, q].rearrange("c (g a) t -> c g (a t)", g=4)).then_inc(m_loaded[q], 16)

            def store_x(itt):
                sp.wait_ge(x2_done, itt + 1)
                sp.nop(nofuse=True)
                sp.dma_start(x_hist[itt + SEQS], x2[:].rearrange("p a b -> p (a b)")).then_inc(x_stored, 16)

            def load_tail_inputs(itt):
                sp.dma_start(xt[:], x_hist[itt].rearrange("p (a b) -> p a b", a=QT)).then_inc(t_loaded, 16)
                sp.dma_start(wt[:], w_tail[itt // SEQS]).then_inc(t_loaded, 16)

            def item(it, par, inner=False):
                tail, tail_end, maxima, projections = runs(it, inner)
                if tail_end:
                    store_x(it - 2)
                if tail:
                    load_tail_inputs(it - 1)
                if maxima:
                    load_value_weights(it + 1)
                if tail_end:
                    sp.wait_ge(x_stored, count(16 * (it - 1)))
                    sp.nop(nofuse=True)
                if projections:
                    load_projection_inputs(it + 2)
                move_maxima(it, par, 3)
                if maxima:
                    move_maxima(it + 1, 1 - par, 0)
                if projections:
                    stage_operands(it + 2, par)
                    load_operands(it + 2, par, 0)
                if maxima:
                    move_maxima(it + 1, 1 - par, 1)
                if projections:
                    load_operands(it + 2, par, 1)
                    load_operands(it + 2, par, 2)
                if maxima:
                    move_maxima(it + 1, 1 - par, 2)
                if projections:
                    load_operands(it + 2, par, 3)

            sp.dma_start(ident[:], ident_d).then_inc(ident_loaded, 16)
            load_value_weights(0)
            for ip in range(2):
                load_projection_inputs(ip)
            for ip in range(2):
                sp.wait_ge((ones_ready, odd_ones_ready)[ip], 2)
                stage_operands(ip, ip)
                for q in range(QUADS):
                    load_operands(ip, ip, q)
            for q in range(QUADS - 1):
                move_maxima(0, 0, q)
            walk(sp, item)
            store_x(ITEMS - 2)
            load_tail_inputs(ITEMS - 1)
            store_x(ITEMS - 1)
            sp.wait_ge(x_stored, 16 * ITEMS)
            sp.nop(nofuse=True)

        @block.tensor
        def _(pe):
            mm, tr = nc.tensor.matmul, nc.tensor.transpose

            def score_t(it, par, s, j):
                g, kt = 4 * (s // 4) + j, s % 4
                t = it * 64 + 4 * s + j
                if kt == 0 and j == 0:
                    pe.wait_ge(m_loaded[s // 4], 16 * (it + 1))
                pe.wait_ge(exp_done, count(t - 1 if par == 0 and s == 0 and j < 2 else t - 2))
                mm(st_ps[st_bank(par, s, j)][:], k_ops[par][0:MROWS, g, kt * P:(kt + 1) * P], q_ops[par][0:MROWS, g, :],
                   start=True, stop=True).then_inc(st_ready, 1)

            def score(im, par, g, qt):
                if qt == 0 and g % 4 == 0:
                    pe.wait_ge(op_loaded[g // 4], 32 * (im + 1))
                pe.wait_ge(s_taken, count(im * 64 + 4 * g + qt - 1))
                mm(s_ps[qt % 2][:], q_ops[par][0:CROWS, g, qt * P:(qt + 1) * P], k_ops[par][0:CROWS, g, :],
                   start=True, stop=True).then_inc(s_ready, 1)

            def weigh_values(n_it, par, s):
                q, kt = s // 4, s % 4
                pe.wait_ge(exp_done, n_it * 64 + 4 * s + 4)
                if s == 0:
                    pe.wait_ge(v_done, n_it + 1)
                if kt == 0:
                    pe.wait_ge(o_copied, n_it * 4 + q)
                for j in range(4):
                    last = mm(o_ps[32 * j:32 * j + VW, :], v_ops[par][:, kt, (4 * q + j) // 2, :],
                              probs[:, s % 4, j, :], start=kt == 0, stop=kt == 3)
                last.then_inc(pv_done, 1)

            def turn_quad(it, q, free, value):
                pe.wait_ge(o_copied, it * 4 + q + 1)
                pe.wait_ge(free, count(value))
                for a in range(QT):
                    last = tr(tail3[:, a, :], oT_raw[:, q % 2, a * P:(a + 1) * P], ident[:])
                last.then_inc(oq_ready, 1)

            def turn_maxima(im, q, free, value):
                pe.wait_ge(s_taken, im * 64 + 16 * (q + 1))
                pe.wait_ge(free, count(value))
                tr(proj_ps[0:16, 0:P], mx[:, q % 2, :], ident[:]).then_inc(mxt_ready, 1)

            def values(iv):
                pe.wait_ge(xt_done, iv + 1)
                pe.wait_ge(wv_loaded, 16 * (iv + 1))
                pe.wait_ge(mr_done, iv * 4)
                for a in range(QT):
                    last = mm(proj3[:, a, :], xT[:, a * P:(a + 1) * P], wv[:], start=True, stop=True)
                last.then_inc(v_ready, 1)

            def turn_x(ip):
                pe.wait_ge(xs_loaded, 16 * (ip + 1))
                pe.wait_ge(v_done, ip)
                for a in range(QT):
                    last = tr(proj3[:, a, :], xs[:, a, :], ident[:])
                last.then_inc(xt_ready, 1)

            def project(ip, which, free, value):
                if which == 0:
                    pe.wait_ge(wqk_loaded, 16 * (ip + 1))
                    pe.wait_ge(xt_done, ip + 1)
                pe.wait_ge(free, count(value))
                mm(proj_ps[:], wqk[:, which, :], xT[:], start=True, stop=True).then_inc((q_ready, k_ready)[which], 1)

            def turn_o(itt):
                pe.wait_ge(o_done, itt + 1)
                pe.wait_ge(oq_taken, 4 * (itt + 1))
                for a in range(QT):
                    last = tr(tail3[:, a, :], o_tok[:, a, :], ident[:])
                last.then_inc(ot_ready, 1)

            def project_o(itt):
                pe.wait_ge(t_loaded, 32 * (itt + 1))
                pe.wait_ge(ot_done, itt + 1)
                for a in range(QT):
                    last = mm(tail3[:, a, :], oT[:, a * P:(a + 1) * P], wt[:, WO0:WO0 + D], start=True, stop=True)
                last.then_inc(wo_ready, 1)

            def turn_h(itt, free, value):
                pe.wait_ge(xn_done, QT * (itt + 1))
                pe.wait_ge(free, count(value))
                for a in range(QT):
                    last = tr(tail3[:, a, :], xn[:, a, :], ident[:])
                last.then_inc(ht_ready, 1)

            def up(itt, j, free, value):
                if j == 0:
                    pe.wait_ge(ht_done, itt + 1)
                pe.wait_ge(free, count(value))
                mm(tail_ps[:], wt[:, W10 + j * P:W10 + (j + 1) * P], hT[:], start=True, stop=True).then_inc(w1_ready, 1)

            def down(itt, free, value):
                pe.wait_ge(gelu_done, itt + 1)
                pe.wait_ge(free, count(value))
                for a in range(QT):
                    for j in range(HT):
                        last = mm(tail3[:, a, :], u[:, j, a * P:(a + 1) * P], wt[:, W20 + j * P:W20 + (j + 1) * P],
                                  start=j == 0, stop=j == HT - 1)
                last.then_inc(w2_ready, 1)

            def tail_alone(itt):
                turn_quad(itt, 2, x2_done, itt)
                turn_quad(itt, 3, oq_taken, itt * 4 + 3)
                turn_o(itt)
                project_o(itt)
                turn_h(itt, x1_done, itt + 1)
                for j in range(HT):
                    up(itt, j, u_in_done if j else ht_done, HT * itt + j if j else itt + 1)
                down(itt, u_in_done, HT * (itt + 1))

            def between(it, par, s, tail, maxima, projections):
                if s == 0:
                    turn_maxima(it, 3, mr_done, it * 4 + 3)
                    if tail:
                        turn_quad(it - 1, 2, x2_done, it - 1)
                if s == 1 and tail:
                    turn_quad(it - 1, 3, oq_taken, it * 4 - 1)
                if s == 2 and maxima:
                    values(it + 1)
                if s == 3 and tail:
                    turn_o(it - 1)
                if s == 4:
                    if tail:
                        project_o(it - 1)
                    if projections:
                        turn_x(it + 2)
                if s == 5 and maxima:
                    turn_maxima(it + 1, 0, xt_done if projections else v_done, it + 3 if projections else it + 2)
                if s == 7:
                    turn_quad(it, 0, x1_done if tail else oq_taken, it)
                    if projections:
                        project(it + 2, 0, mr_done, it * 4 + 5)
                if s == 9:
                    turn_quad(it, 1, oq_taken, it * 4 + 1)
                    if projections:
                        project(it + 2, 1, qr_done, it + 3)
                if s == 10 and tail:
                    turn_h(it - 1, oq_taken, it * 4 + 2)
                if s == 11:
                    if tail:
                        up(it - 1, 0, ht_done, it)
                    if maxima:
                        turn_maxima(it + 1, 1, kr_done if projections else mr_done,
                                    it + 3 if projections else it * 4 + 5)
                if s in (12, 13, 14) and tail:
                    up(it - 1, s - 11, u_in_done, it * 4 - 15 + s)
                if s == 13 and maxima:
                    turn_maxima(it + 1, 2, mr_done, it * 4 + 6)

            def item(it, par, inner=False):
                tail, tail_end, maxima, projections = runs(it, inner)
                for s in range(STEPS):
                    last = s == STEPS - 1
                    if maxima:
                        score(it + 1, 1 - par, s, 0)
                    score_t(it, par, s, 0)
                    score_t(it, par, s, 1)
                    if maxima:
                        score(it + 1, 1 - par, s, 1)
                    score_t(it, par, s, 2)
                    if not last:
                        score_t(it, par, s, 3)
                    if maxima:
                        score(it + 1, 1 - par, s, 2)
                    if s != 3:
                        between(it, par, s, tail, maxima, projections)
                    if s > 0:
                        weigh_values(it, par, s - 1)
                    elif tail:
                        weigh_values(it - 1, 1 - par, STEPS - 1)
                    if s == 3:
                        between(it, par, s, tail, maxima, projections)
                    if maxima:
                        score(it + 1, 1 - par, s, 3)
                    if last:
                        if tail:
                            down(it - 1, u_in_done, it * 4)
                        score_t(it, par, s, 3)

            pe.wait_ge(ident_loaded, 16)
            for ip in range(2):
                if ip == 0:
                    turn_x(0)
                else:
                    pe.wait_ge(kr_done, 1)
                    values(0)
                    turn_x(1)
                project(ip, 0, kr_done, ip)
                project(ip, 1, qr_done, ip + 1)
            for q in range(QUADS):
                for g in range(4 * q, 4 * q + 4):
                    for a in range(QT):
                        score(0, 0, g, a)
                if q < QUADS - 1:
                    turn_maxima(0, q, kr_done if q == 0 else mr_done, 2 if q == 0 else q)
            walk(pe, item)
            weigh_values(ITEMS - 1, 1, STEPS - 1)
            tail_alone(ITEMS - 1)

        @block.scalar
        def _(act):
            A = nc.scalar.activation

            def exps(it, par, s, j):
                t = it * 64 + 4 * s + j
                act.wait_ge(st_ready, t + 1)
                if j == 0:
                    act.wait_ge(pv_done, count(it * 16 + s - 3))
                A(probs[:, s % 4, j, :], st_ps[st_bank(par, s, j)][:], ACT.Exp, scale=SCALE).then_inc(exp_done, 1)

            def copy_quad(it, q):
                act.wait_ge(pv_done, it * 16 + 4 * (q + 1))
                act.wait_ge(oq_ready, count(it * 4 + q - 1))
                nc.scalar.copy(oT_raw[:, q % 2, :], o_ps[:]).then_inc(o_copied, 1)

            def m_first(im, q):
                act.wait_ge(mxt_ready, im * 4 + q + 1)
                act.wait_ge(m_written, count(16 * (im * 4 + q - 1)))
                A(m_parts[:, q % 2, 0, :], proj_ps[0:16, 0:P], ACT.Copy, scale=-1.0).then_inc(m1_done, 1)

            def m_second(im, q):
                act.wait_ge(mr_done, im * 4 + q + 1)
                nc.scalar.copy(m_parts[:, q % 2, 1, :], m_rest[:, q % 2, :]).then_inc(m2_done, 1)

            def copy_x(ip):
                act.wait_ge(xt_ready, ip + 1)
                act.wait_ge(v_ready, ip)
                act.wait_ge(k_ready, ip)
                nc.scalar.copy(xT[:], proj_ps[:]).then_inc(xt_done, 1)

            def first_part(ip, which):
                act.wait_ge((q_ready, k_ready)[which], count(ip + 1))
                act.wait_ge(qk_written, 2 * COMBOS * 16 * ip)
                nc.scalar.copy(parts[:, which, 0, :], proj_ps[:]).then_inc((q1_done, k1_done)[which], 1)

            def second_part(ip, which):
                act.wait_ge((qr_done, kr_done)[which], count(ip + 1))
                nc.scalar.copy(parts[:, which, 1, :], rest[:, which, :]).then_inc((q2_done, k2_done)[which], 1)

            def squares(itt):
                act.wait_ge(o_done, itt + 1)
                act.wait_ge(sq_done, QT * itt)
                act.wait_ge(ms_done, itt)
                for a in range(QT):
                    A(junk[:, a, :], o_tok[:, a, :], ACT.Square, accum_out=sumsq[:, a:a + 1]).then_inc(sq_done, 1)

            def scale_o(itt):
                act.wait_ge(ot_ready, itt + 1)
                act.wait_ge(t_loaded, 32 * (itt + 1))
                A(oT[:], tail_ps[:], ACT.Copy, scale=wt[:, RW0:RW0 + 1]).then_inc(ot_done, 1)

            def affine_h(itt):
                act.wait_ge(ht_ready, itt + 1)
                A(hT[:], tail_ps[:], ACT.Identity, scale=wt[:, G0:G0 + 1], bias=wt[:, B0:B0 + 1]).then_inc(ht_done, 1)

            def hidden(itt, j):
                act.wait_ge(w1_ready, HT * itt + j + 1)
                if j == 0:
                    act.wait_ge(gelu_done, itt)
                A(u_in[:, j, :], tail_ps[:], ACT.Identity, bias=wt[:, B10 + j:B10 + j + 1]).then_inc(u_in_done, 1)

            def gelus(itt):
                act.wait_ge(u_in_done, HT * (itt + 1))
                act.wait_ge(w2_ready, itt)
                A(u[:], u_in[:], ACT.Gelu).then_inc(gelu_done, 1)

            def item(it, par, inner=False):
                tail, tail_end, maxima, projections = runs(it, inner)
                for s in range(STEPS):
                    exps(it, par, s, 0)
                    if s == 1 and tail:
                        copy_quad(it - 1, 3)
                    if s == 4 and tail:
                        scale_o(it - 1)
                    if s in (5, 9, 13):
                        copy_quad(it, s // 4 - 1)
                    for j in range(1, 4):
                        exps(it, par, s, j)
                    if s == 0:
                        m_first(it, 3)
                    if s == 1:
                        m_second(it, 3)
                    if s == 3 and tail:
                        squares(it - 1)
                    if s == 4 and projections:
                        copy_x(it + 2)
                    if s == 5 and maxima:
                        m_first(it + 1, 0)
                    if s == 6 and maxima:
                        m_second(it + 1, 0)
                    if s == 7 and projections:
                        first_part(it + 2, 0)
                    if s == 8 and projections:
                        second_part(it + 2, 0)
                    if s == 9 and projections:
                        first_part(it + 2, 1)
                    if s == 10:
                        if tail:
                            affine_h(it - 1)
                        if projections:
                            second_part(it + 2, 1)
                    if s in (11, 13) and maxima:
                        m_first(it + 1, s // 2 - 4)
                    if s in (11, 12, 13, 14) and tail:
                        hidden(it - 1, s - 11)
                    if s in (12, 14) and maxima:
                        m_second(it + 1, s // 2 - 5)
                    if s == 14 and tail:
                        gelus(it - 1)

            for ip in range(2):
                copy_x(ip)
                for which in range(2):
                    first_part(ip, which)
                    second_part(ip, which)
            for q in range(QUADS - 1):
                m_first(0, q)
                m_second(0, q)
            walk(act, item)
            last = ITEMS - 1
            copy_quad(last, 3)
            squares(last)
            scale_o(last)
            affine_h(last)
            for j in range(HT):
                hidden(last, j)
            gelus(last)

        @block.vector
        def _(dve):
            V = nc.vector

            def maximum(im, g, qt):
                t = im * 64 + 4 * g + qt
                dve.wait_ge(s_ready, t + 1)
                if g % 4 == 0 and qt == 0:
                    dve.wait_ge(mxt_ready, count(im * 4 + g // 4 - 1))
                c = 4 * (g % 4) + qt
                V.reduce_max(mx[:, (g // 4) % 2, c:c + 1], s_ps[qt % 2][:], AX.X).then_inc(s_taken, 1)

            def m_remainder(im, q):
                dve.wait_ge(m1_done, im * 4 + q + 1)
                dve.wait_ge(m3_done, count(im * 4 + q - 1))
                V.scalar_tensor_tensor(out=m_rest[:, q % 2, :], in0=proj_ps[0:16, 0:P], scalar=-1.0,
                                       in1=m_parts[:, q % 2, 0, :], op0=ALU.mult, op1=ALU.subtract).then_inc(mr_done, 1)

            def remainder(ip, which):
                dve.wait_ge((q1_done, k1_done)[which], count(ip + 1))
                dve.wait_ge((q3_done, k3_done)[which], count(ip))
                V.tensor_tensor(rest[:, which, :], proj_ps[:], parts[:, which, 0, :],
                                ALU.subtract).then_inc((qr_done, kr_done)[which], 1)

            def keep_values(iv, par):
                dve.wait_ge(v_ready, iv + 1)
                dve.wait_ge(pv_done, count(16 * (iv - 1)))
                V.tensor_copy(v_ops[par][:, :, :, 0:E],
                              proj_ps[:].rearrange("p (a h e) -> p a h e", a=QT, h=HEADS)).then_inc(v_done, 1)

            def normalise(it, q):
                src = tail_ps[:].rearrange("p (a j w) -> p a j w", a=QT, j=4)
                dve.wait_ge(oq_ready, it * 4 + q + 1)
                V.reciprocal(rz[:, q % 2, :, :], src[:, :, :, E]).then_inc(rz_done, 1)
                dve.wait_ge(rz_done, it * 4 + q + 1)
                if q == 0:
                    dve.wait_ge(o_done, it)
                dst = o_norm[:].rearrange("p (a q h) i e -> p a q (h i) e", a=QT, q=QUADS)[:, :, q]
                V.tensor_tensor(dst, src[:, :, :, 0:E], rz[:, q % 2, :, :].unsqueeze(3).to_broadcast([P, QT, 4, E]),
                                ALU.mult).then_inc(oq_taken, 1)

            def add_attention(itt, tiles):
                if tiles[0] == 0:
                    dve.wait_ge(wo_ready, itt + 1)
                    dve.wait_ge(rms_done, itt + 1)
                    dve.wait_ge(xb_done, itt + 1)
                    dve.wait_ge(x1b_done, itt)
                    dve.wait_ge(xn_done, QT * itt)
                for a in tiles:
                    last = V.scalar_tensor_tensor(out=x1[:, a, :], in0=tail3[:, a, :], scalar=rms[:, a:a + 1],
                                                  in1=xb[:, a, :], op0=ALU.mult, op1=ALU.add)
                if tiles[-1] == QT - 1:
                    last.then_inc(x1_done, 1)

            def statistics(itt):
                dve.wait_ge(x1_done, itt + 1)
                for a in range(QT):
                    last = V.bn_stats(stats[:, a, :], x1[:, a, :])
                last.then_inc(bn_done, 1)

            def moments(itt):
                dve.wait_ge(bn_done, itt + 1)
                dve.nop(nofuse=True)
                for a in range(QT):
                    last = V.bn_aggr(mv[:, a, :], stats[:, a, :])
                last.then_inc(mv_done, 1)

            def add_mlp(itt):
                dve.wait_ge(w2_ready, itt + 1)
                dve.wait_ge(x1b_done, itt + 1)
                dve.wait_ge(x_stored, 16 * itt)
                V.tensor_tensor(x2[:], tail3[:], x1b[:], ALU.add).then_inc(x2_done, 1)

            def item(it, par, inner=False):
                tail, tail_end, maxima, projections = runs(it, inner)
                for s in range(STEPS):
                    if maxima:
                        maximum(it + 1, s, 0)
                        maximum(it + 1, s, 1)
                    if s == 6 and tail:
                        add_attention(it - 1, (2, 3))
                    if s == 7 and tail:
                        statistics(it - 1)
                    if s == 8 and tail:
                        moments(it - 1)
                    if maxima:
                        maximum(it + 1, s, 2)
                    if s == 0 and tail:
                        normalise(it - 1, 2)
                    if s == 1:
                        m_remainder(it, 3)
                        if tail:
                            normalise(it - 1, 3)
                    if s == 2 and maxima:
                        keep_values(it + 1, 1 - par)
                    if s == 5 and tail:
                        add_attention(it - 1, (0, 1))
                    if s == 6 and maxima:
                        m_remainder(it + 1, 0)
                    if s == 7:
                        normalise(it, 0)
                    if s == 8 and projections:
                        remainder(it + 2, 0)
                    if s == 9:
                        normalise(it, 1)
                    if s == 10 and projections:
                        remainder(it + 2, 1)
                    if s in (12, 14) and maxima:
                        m_remainder(it + 1, s // 2 - 5)
                    if maxima:
                        maximum(it + 1, s, 3)
                if tail:
                    add_mlp(it - 1)

            V.memset(k_ops[0][32:64, :, :], 1.0).then_inc(ones_ready, 1)
            V.memset(q_ops[0][32:64, :, :], 0.0).then_inc(ones_ready, 1)
            for i in range(2):
                V.memset(v_ops[i][:], 0.0).then_inc(const_ready, 1)
            dve.wait_ge(const_ready, 2)
            for i in range(2):
                V.memset(v_ops[i][:, :, :, E:E + 1], 1.0).then_inc(const_ready, 1)
            dve.wait_ge(const_ready, 4)
            for ip in range(2):
                if ip == 1:
                    keep_values(0, 0)
                remainder(ip, 0)
                remainder(ip, 1)
            for q in range(QUADS):
                for g in range(4 * q, 4 * q + 4):
                    for a in range(QT):
                        maximum(0, g, a)
                if q < QUADS - 1:
                    m_remainder(0, q)
            walk(dve, item)
            normalise(ITEMS - 1, 2)
            normalise(ITEMS - 1, 3)
            add_attention(ITEMS - 1, (0, 1, 2, 3))
            statistics(ITEMS - 1)
            moments(ITEMS - 1)
            add_mlp(ITEMS - 1)

        @block.gpsimd
        def _(pool):
            G = nc.gpsimd

            def third_part(ip, which):
                pool.wait_ge((q2_done, k2_done)[which], count(ip + 1))
                pool.nop(nofuse=True)
                G.tensor_tensor(parts[:, which, 2, :], rest[:, which, :], parts[:, which, 1, :],
                                ALU.subtract).then_inc((q3_done, k3_done)[which], 1)

            def m_third(im, q):
                pool.wait_ge(m2_done, im * 4 + q + 1)
                pool.nop(nofuse=True)
                G.tensor_tensor(m_parts[:, q % 2, 2, :], m_rest[:, q % 2, :], m_parts[:, q % 2, 1, :],
                                ALU.subtract).then_inc(m3_done, 1)

            def prepare(itt):
                pool.wait_ge(t_loaded, 32 * (itt + 1))
                pool.nop(nofuse=True)
                G.tensor_scalar(omd[:], wt[:, DW0:DW0 + 1], -1.0, 1.0, ALU.mult, ALU.add).then_inc(omd_done, 1)
                G.tensor_scalar(ndw[:], wt[:, DW0:DW0 + 1], -1.0, None, ALU.mult).then_inc(omd_done, 1)
                pool.wait_ge(omd_done, 2 * (itt + 1))
                pool.nop(nofuse=True)
                G.tensor_scalar(bos[:], wt[:, BO0:BO0 + D], omd[:], None, ALU.mult).then_inc(bos_done, 1)
                pool.wait_ge(bos_done, itt + 1)
                pool.nop(nofuse=True)
                pool.wait_ge(x1_done, itt)
                pool.nop(nofuse=True)
                G.tensor_tensor(xb[:], xt[:], bos[:].unsqueeze(1).to_broadcast([P, QT, D]), ALU.add).then_inc(xb_done, 1)

            def combine(itt):
                pool.wait_ge(oq_taken, 4 * (itt + 1))
                pool.nop(nofuse=True)
                G.tensor_scalar(o_neg[:], o_norm[:, :, 1, :], ndw[:], None, ALU.mult).then_inc(neg_done, 1)
                pool.wait_ge(neg_done, itt + 1)
                pool.nop(nofuse=True)
                pool.wait_ge(ot_ready, itt)
                pool.nop(nofuse=True)
                pool.wait_ge(sq_done, QT * itt)
                pool.nop(nofuse=True)
                G.tensor_tensor(o_tok[:].rearrange("p a (h e) -> p (a h) e", h=HEADS), o_norm[:, :, 0, :], o_neg[:],
                                ALU.add).then_inc(o_done, 1)

            def root_mean(itt):
                pool.wait_ge(sq_done, QT * (itt + 1))
                pool.nop(nofuse=True)
                G.tensor_scalar(rms[:], sumsq[:], 1.0 / D, RMS_EPS, ALU.mult, ALU.add).then_inc(ms_done, 1)
                pool.wait_ge(ms_done, itt + 1)
                pool.nop(nofuse=True)
                G.tensor_tensor(rms[:], rms[:], half[:], ALU.pow).then_inc(pow_done, 1)
                pool.wait_ge(pow_done, itt + 1)
                pool.nop(nofuse=True)
                G.tensor_scalar(rms[:], rms[:], omd[:], None, ALU.mult).then_inc(rms_done, 1)

            def norm_x(itt):
                pool.wait_ge(mv_done, itt + 1)
                pool.nop(nofuse=True)
                G.tensor_scalar(rstd[:], mv[:, :, 1], LN_EPS, None, ALU.add).then_inc(ve_done, 1)
                pool.wait_ge(ve_done, itt + 1)
                pool.nop(nofuse=True)
                G.tensor_tensor(rstd[:], rstd[:], half[:], ALU.pow).then_inc(rs_done, 1)
                pool.wait_ge(rs_done, itt + 1)
                pool.nop(nofuse=True)
                pool.wait_ge(ht_ready, itt)
                pool.nop(nofuse=True)
                for a in range(QT):
                    G.tensor_scalar(xn[:, a, :], x1[:, a, :], mv[:, a, 0:1], rstd[:, a:a + 1],
                                    ALU.subtract, ALU.mult).then_inc(xn_done, 1)
                pool.wait_ge(x2_done, itt)
                pool.nop(nofuse=True)
                G.tensor_tensor(x1b[:], x1[:], wt[:, B20:B20 + D].unsqueeze(1).to_broadcast([P, QT, D]),
                                ALU.add).then_inc(x1b_done, 1)

            def item(it, par, inner=False):
                tail, tail_end, maxima, projections = runs(it, inner)
                if tail:
                    prepare(it - 1)
                    combine(it - 1)
                m_third(it, 3)
                if tail:
                    root_mean(it - 1)
                if maxima:
                    m_third(it + 1, 0)
                if tail:
                    norm_x(it - 1)
                if projections:
                    third_part(it + 2, 0)
                    third_part(it + 2, 1)
                if maxima:
                    m_third(it + 1, 1)
                    m_third(it + 1, 2)

            G.memset(half[:], -0.5).then_inc(half_ready, 1)
            pool.wait_ge(half_ready, 1)
            G.memset(k_ops[1][32:64, :, :], 1.0).then_inc(odd_ones_ready, 1)
            pool.wait_ge(odd_ones_ready, 1)
            G.memset(q_ops[1][32:64, :, :], 0.0).then_inc(odd_ones_ready, 1)
            pool.wait_ge(odd_ones_ready, 2)
            pool.nop(nofuse=True)
            for ip in range(2):
                third_part(ip, 0)
                third_part(ip, 1)
            for q in range(QUADS - 1):
                m_third(0, q)
            walk(pool, item)
            last = ITEMS - 1
            prepare(last)
            combine(last)
            root_mean(last)
            norm_x(last)
VOCAB = 8000
TAPS = 3
S_KEYS = 250
KT0 = S_KEYS // 2
D_LLM = 1024
LC = D_LLM // P
CROWS0 = COMBOS * E
MROWS0 = CROWS0 + PARTS
SCALE0 = float(E) ** -0.5
GE = 160
OPS3 = 3
NF = 8
ROUND = 12582912.0

WQ0, WOA0, BQ0, BK0 = 0, D, 2 * D, 2 * D + 1
BV0, BOA0 = 2 * D + 2, 3 * D + 2
W2G0 = 4 * D + 2
B2G0 = W2G0 + OPS3 * GE
FIRST0 = B2G0 + OPS3
IOTA0 = FIRST0 + 64
APAR = IOTA0 + 32


def embed_attend_gate(nc, ids, taps, src_t, val_t, w_kv, par_d, w_gate_d, ident_d, x_hist, h_hist,
                      scr_q, scr_k, scr_m):
    with ExitStack() as ctx:
        def sb(name, shape, dt=F32):
            return ctx.enter_context(nc.sbuf_tensor(name, shape, dt))

        def sem(name):
            return ctx.enter_context(nc.semaphore(name))

        ident = sb("t_ident", [P, P])
        par = sb("t_par", [P, APAR])
        w_gate = sb("w_gate", [NF, 2, OPS3 * GE])
        gate_parts = sb("gate_parts", [NF, PARTS, 2, OPS3 * GE], BF16)
        gate_rest = sb("gate_rest", [NF, 2, OPS3 * GE])
        gate_ops = sb("gate_ops", [COMBOS * NF, 2, OPS3 * GE], BF16)
        srcT = sb("srcT", [P, LC, S_KEYS])
        valT = sb("valT", [P, LC, S_KEYS])
        wkv = sb("wkv", [P, 2, LC, D])
        idx = sb("idx", [P, TAPS * QT], I32)
        taps_in = sb("taps_in", [P, TAPS, QT, D])
        h0 = sb("h0", [P, QT, D])
        hb = [sb(f"hb{i}", [P, QT, D]) for i in range(2)]
        h1 = sb("h1", [P, QT, D])
        h2 = sb("h2", [P, QT, D])
        x_bd = sb("x_bd", [P, QT, D])
        y_tok = sb("y_tok", [P, QT, D])
        x_out = sb("x_out", [P, QT, D])
        yT = sb("yT", [P, TOK])
        stats = sb("t_stats", [P, QT, 6])
        mv = sb("t_mv", [P, QT, 2])
        rstd = sb("t_rstd", [P, QT])
        half = sb("t_half", [P, QT])
        qf = sb("qf", [P, TOK])
        q_parts = sb("q_parts", [P, PARTS, TOK], BF16)
        q_rest = sb("q_rest", [P, TOK])
        kf = sb("kf", [P, S_KEYS])
        k_parts = sb("k_parts", [P, PARTS, S_KEYS], BF16)
        k_rest = sb("k_rest", [P, S_KEYS])
        q_ops = [sb(f"t_q_ops{i}", [P, HEADS, TOK], BF16) for i in range(2)]
        k_ops = sb("t_k_ops", [P, HEADS, S_KEYS], BF16)
        v_ops = sb("t_v_ops", [P, 2, HEADS, VW])
        mx = sb("t_mx", [P, HEADS * QT])
        m_parts = sb("t_m_parts", [32, PARTS, P], BF16)
        m_rest = sb("t_m_rest", [32, P])
        probs = sb("t_probs", [P, 2, 4, TOK])
        oT_raw = sb("t_oT_raw", [P, 2, TOK])
        rz = sb("t_rz", [P, 2, QT, 4])
        o_tok = sb("t_o_tok", [P, QT, D])
        oT = sb("t_oT", [P, TOK])
        bits = sb("bits", [P, QT, 64])
        first = sb("first", [P, QT * 4])
        left = sb("left", [P, QT * 4])
        feat = sb("feat", [P, QT, NF])
        feat_parts = sb("feat_parts", [P, QT, 2, NF], BF16)
        feat_rest = sb("feat_rest", [P, QT, NF])
        feat_ops = sb("feat_ops", [P, QT, COMBOS, NF])
        fT = sb("fT", [COMBOS * NF, TOK], BF16)
        gated = sb("gated", [P, 2, OPS3 * GE])
        y = sb("gate_y", [P, QT, 2, OPS3])
        ysel = sb("ysel", [P, QT, 2, OPS3])
        on = sb("on", [P, QT, 3])
        off = sb("off", [P, QT, 3])
        pick = sb("pick", [P, QT, 3])
        any_on = sb("any_on", [P, QT])
        mark = sb("mark", [P, QT])
        res = sb("res", [P, QT, 2])
        hot = sb("hot", [P, QT, 2, 16])

        s_ps = [ctx.enter_context(nc.psum_tensor(f"t_s_ps{i}", [P, TOK], F32)) for i in range(2)]
        st_ps = [ctx.enter_context(nc.psum_tensor(f"t_st_ps{i}", [P, TOK], F32)) for i in range(2)]
        o_ps = [ctx.enter_context(nc.psum_tensor(f"t_o_ps{i}", [P, TOK], F32)) for i in range(2)]
        work_a = ctx.enter_context(nc.psum_tensor("t_work_a", [P, TOK], F32))
        work_b = ctx.enter_context(nc.psum_tensor("t_work_b", [P, TOK], F32))
        work3 = work_b[:, :].rearrange("p (a b) -> p a b", a=QT)

        (loaded, gathered, idx_loaded, h0_done, k_ready, v_ready, kv_done, kparts_done, k_stored, k_loaded,
         ones_done, half_done, stats_done, mv_done, rstd_done, norm_done, y_turned, yT_done, turned, turn_taken, q_ready, q_first, q_rest_done,
         q_second, q_third, q_stored, q_loaded, s_ready, s_taken, mxt_ready, m_first, m_rest_done, m_second,
         m_third, m_stored, m_loaded, st_ready, exp_done, pv_done, o_copied, oq_ready, oq_taken, wo_ready,
         hb_done, h1_done, feat_done, hid_ready, hid_taken, h2_done, h_stored, x_done,
         x_stored, conv_step, gate_step, pool_step, qf_done, gate_split, gates_loaded) = [sem("t_" + n) for n in (
             "loaded gathered idx_loaded h0_done k_ready v_ready kv_done kparts_done k_stored k_loaded "
             "ones_done half_done stats_done mv_done rstd_done norm_done y_turned yT_done turned turn_taken q_ready q_first q_rest_done "
             "q_second q_third q_stored q_loaded s_ready s_taken mxt_ready m_first m_rest_done m_second "
             "m_third m_stored m_loaded st_ready exp_done pv_done o_copied oq_ready oq_taken wo_ready "
             "hb_done h1_done feat_done hid_ready hid_taken h2_done h_stored x_done "
             "x_stored conv_step gate_step pool_step qf_done gate_split gates_loaded").split()]
        block = ctx.enter_context(nc.Block())
        LOADS = 7

        def turns(eng, turn):
            turn(0, None, None, 0, 1, 2)
            turn(1, 0, None, 1, 2, 2)
            turn(2, 1, 0, 0, 3, 2)
            turn(3, 2, 1, 1, 6, 2)
            with eng.Fori(2, SEQS // 2 - 1) as pair:
                for par in range(2):
                    turn(pair * 2 + par, pair * 2 + (par - 1), pair * 2 + (par - 2), par, pair * 6 + (3 * par - 3), 2)
            turn(SEQS - 2, SEQS - 3, SEQS - 4, 0, 3 * SEQS - 9, 1)
            turn(SEQS - 1, SEQS - 2, SEQS - 3, 1, 3 * SEQS - 6, 0)
            turn(None, SEQS - 1, SEQS - 2, 0, 3 * SEQS - 4, 0)
            turn(None, None, SEQS - 1, 1, 3 * SEQS - 2, 0)

        @block.sync
        def _(sp):
            for dst, src in ((idx[:], ids[0]), (ident[:], ident_d), (par[:], par_d), (w_gate[:], w_gate_d),
                             (srcT[:], src_t), (valT[:], val_t), (wkv[:], w_kv)):
                sp.dma_start(dst, src).then_inc(idx_loaded if dst.tensor is idx[:].tensor else loaded, 16)
            sp.wait_ge(gate_split, 4)
            for c in range(COMBOS):
                sp.dma_start(gate_ops[c * NF:(c + 1) * NF], gate_parts[:, K_PART[c]]).then_inc(gates_loaded, 16)
            sp.wait_ge(kparts_done, 1)
            sp.nop(nofuse=True)
            for c in range(COMBOS):
                sp.dma_start(scr_k[c], k_parts[:, K_PART[c], :]).then_inc(k_stored, 16)
            sp.wait_ge(k_stored, 16 * COMBOS)
            sp.nop(nofuse=True)
            sp.wait_ge(ones_done, 2)
            sp.nop(nofuse=True)
            sp.dma_start(k_ops[0:CROWS0], scr_k.rearrange("c (e h) t -> (c e) h t", h=HEADS)).then_inc(k_loaded, 16)

            sp.wait_ge(gathered, 16 * TAPS * QT)
            sp.nop(nofuse=True)
            sp.dma_start(idx[:], ids[1]).then_inc(idx_loaded, 16)

            def turn(a, m, b, pa, roots, more):
                if more > 1:
                    sp.wait_ge(gathered, 16 * TAPS * QT * (a + 2))
                    sp.nop(nofuse=True)
                    sp.dma_start(idx[:], ids[a + 2]).then_inc(idx_loaded, 16)
                if a is not None:
                    sp.wait_ge(q_third, a + 1)
                    sp.nop(nofuse=True)
                    for c in range(COMBOS):
                        sp.dma_start(scr_q[c], q_parts[:, Q_PART[c], :]).then_inc(q_stored, 16)
                    sp.wait_ge(q_stored, 16 * COMBOS * (a + 1))
                    sp.nop(nofuse=True)
                    sp.wait_ge(st_ready, count(16 * (a - 1)))
                    sp.nop(nofuse=True)
                    sp.dma_start(q_ops[pa][0:CROWS0], scr_q.rearrange("c (e h) t -> (c e) h t", h=HEADS)).then_inc(q_loaded, 16)
                if m is not None:
                    sp.wait_ge(m_third, m + 1)
                    sp.nop(nofuse=True)
                    sp.dma_start(scr_m.rearrange("c p t -> p c t"), m_parts[:]).then_inc(m_stored, 16)
                    sp.wait_ge(m_stored, 16 * (m + 1))
                    sp.nop(nofuse=True)
                    sp.dma_start(q_ops[1 - pa][CROWS0:MROWS0], scr_m.rearrange("c (h a) t -> c h (a t)", h=HEADS)).then_inc(m_loaded, 16)
                if b is not None:
                    sp.wait_ge(h2_done, b + 1)
                    sp.nop(nofuse=True)
                    sp.dma_start(h_hist[b], h2[:].rearrange("p a b -> p (a b)")).then_inc(h_stored, 16)
                    sp.wait_ge(x_done, b + 1)
                    sp.nop(nofuse=True)
                    sp.dma_start(x_hist[b], x_out[:].rearrange("p a b -> p (a b)")).then_inc(x_stored, 16)

            turns(sp, turn)
            sp.wait_ge(h_stored, 16 * SEQS)
            sp.nop(nofuse=True)
            sp.wait_ge(x_stored, 16 * SEQS)
            sp.nop(nofuse=True)

        @block.tensor
        def _(pe):
            mm, tr = nc.tensor.matmul, nc.tensor.transpose
            pe.wait_ge(loaded, 16 * (LOADS - 1))
            for c in range(LC):
                last = mm(work_a[:, 0:S_KEYS], wkv[:, 0, c, :], srcT[:, c, :], start=c == 0, stop=c == LC - 1)
            last.then_inc(k_ready, 1)
            for kt in range(2):
                for c in range(LC):
                    last = mm(s_ps[kt][0:KT0, 0:D], valT[:, c, kt * KT0:(kt + 1) * KT0], wkv[:, 1, c, :],
                              start=c == 0, stop=c == LC - 1)
            last.then_inc(v_ready, 1)
            pe.wait_ge(kv_done, 3)
            pe.wait_ge(k_loaded, 16)
            pe.wait_ge(gates_loaded, 16 * COMBOS)

            def flip(dst, src, n=P):
                for a in range(QT):
                    last = tr(dst[0:n, a * P:(a + 1) * P], src[:, a, :], ident[:])
                return last

            def score(m, par, n, tile):
                if n == 0 and tile == 0:
                    pe.wait_ge(q_loaded, 16 * (m + 1))
                    pe.wait_ge(hid_taken, count((m - 1) * 2 * QT))
                t = n * QT + tile
                pe.wait_ge(s_taken, count(m * 16 + t - 1))
                for i in range(2):
                    h = 2 * n + i
                    last = mm(s_ps[t % 2][:, i * S_KEYS:(i + 1) * S_KEYS], q_ops[par][0:CROWS0, h, tile * P:(tile + 1) * P],
                              k_ops[0:CROWS0, h, :], start=True, stop=True)
                last.then_inc(s_ready, 1)

            def score_t(b, par, n, j):
                q, kt = n // 2, n % 2
                h = 4 * q + j
                pe.wait_ge(exp_done, count(b * 16 + 4 * n + j - 1))
                mm(st_ps[j % 2][0:KT0, :], k_ops[0:MROWS0, h, kt * KT0:(kt + 1) * KT0], q_ops[par][0:MROWS0, h, :],
                   start=True, stop=True).then_inc(st_ready, 1)

            def both(m, b, pa, n):
                for j in range(4):
                    if b is not None:
                        score_t(b, pa, n, j)
                    if m is not None:
                        score(m, 1 - pa, n, j)

            def weigh(b, n):
                q, kt = n // 2, n % 2
                pe.wait_ge(exp_done, b * 16 + 4 * n + 4)
                if kt == 0:
                    pe.wait_ge(o_copied, 2 * b)
                for j in range(4):
                    last = mm(o_ps[q][32 * j:32 * j + VW, :], v_ops[0:KT0, kt, 4 * q + j, :],
                              probs[0:KT0, n % 2, j, :], start=kt == 0, stop=kt == 1)
                last.then_inc(pv_done, 1)

            def turn(a, m, b, pa, roots, more):
                if b is not None:
                    pe.wait_ge(m_loaded, 16 * (b + 1))
                both(m, b, pa, 0)
                if a is not None:
                    pe.wait_ge(norm_done, a + 1)
                    flip(work_a, y_tok).then_inc(y_turned, 1)
                both(m, b, pa, 1)
                if b is not None:
                    weigh(b, 0)
                if a is not None:
                    pe.wait_ge(yT_done, a + 1)
                    mm(work_a[:], par[:, WQ0:WQ0 + D], yT[:], start=True, stop=True).then_inc(q_ready, 1)
                both(m, b, pa, 2)
                if b is not None:
                    weigh(b, 1)
                both(m, b, pa, 3)
                if b is not None:
                    weigh(b, 2)
                    weigh(b, 3)
                if m is not None:
                    pe.wait_ge(s_taken, (m + 1) * 16)
                    if a is not None:
                        pe.wait_ge(qf_done, a + 1)
                    tr(work_a[0:HEADS * QT, 0:P], mx[:], ident[:]).then_inc(mxt_ready, 1)
                if b is not None:
                    for q in range(2):
                        pe.wait_ge(o_copied, 2 * b + q + 1)
                        pe.wait_ge(oq_taken, 2 * b + q)
                        flip(work_b, oT_raw[:, q, :].rearrange("p (a t) -> p a t", a=QT)).then_inc(oq_ready, 1)
                    pe.wait_ge(oq_taken, 2 * b + 2)
                    flip(work_b, o_tok).then_inc(turned, 1)
                    pe.wait_ge(turn_taken, 2 * b + 1)
                    for tile in range(QT):
                        last = mm(work3[:, tile, :], oT[:, tile * P:(tile + 1) * P], par[:, WOA0:WOA0 + D], start=True, stop=True)
                    last.then_inc(wo_ready, 1)
                    pe.wait_ge(feat_done, b + 1)
                    pe.nop(nofuse=True)
                    flip(work_b, feat_ops[:].rearrange("p a c n -> p a (c n)"), COMBOS * NF).then_inc(turned, 1)
                    pe.wait_ge(turn_taken, 2 * b + 2)
                    for t in range(2 * QT):
                        tile, i = t // 2, t % 2
                        pe.wait_ge(hid_taken, count(b * 2 * QT + t - 1))
                        mm(s_ps[i][:, 0:OPS3 * GE], fT[:, tile * P:(tile + 1) * P], gate_ops[:, i, :],
                           start=True, stop=True).then_inc(hid_ready, 1)

            turns(pe, turn)

        @block.scalar
        def _(act):
            A, copy = nc.scalar.activation, nc.scalar.copy
            act.wait_ge(loaded, 16 * (LOADS - 1))
            act.wait_ge(k_ready, 1)
            A(kf[:], work_a[:, 0:S_KEYS], ACT.Identity, bias=par[:, BK0:BK0 + 1]).then_inc(kv_done, 1)

            def exps(b, n):
                if n > 0:
                    act.wait_ge(pv_done, count(4 * b + n - 1))
                for j in range(4):
                    act.wait_ge(st_ready, b * 16 + 4 * n + j + 1)
                    A(probs[0:KT0, n % 2, j, :], st_ps[j % 2][0:KT0, :], ACT.Exp, scale=SCALE0).then_inc(exp_done, 1)

            def turn(a, m, b, pa, roots, more):
                if b is not None:
                    exps(b, 0)
                if a is not None:
                    act.wait_ge(y_turned, a + 1)
                    copy(yT[:], work_a[:]).then_inc(yT_done, 1)
                if b is not None:
                    exps(b, 1)
                if a is not None:
                    act.wait_ge(q_ready, a + 1)
                    A(qf[:], work_a[:], ACT.Identity, bias=par[:, BQ0:BQ0 + 1]).then_inc(qf_done, 1)
                    act.wait_ge(qf_done, a + 1)
                    act.wait_ge(q_stored, 16 * COMBOS * a)
                    copy(q_parts[:, 0, :], qf[:]).then_inc(q_first, 1)
                if b is not None:
                    exps(b, 2)
                if a is not None:
                    act.wait_ge(q_rest_done, a + 1)
                    copy(q_parts[:, 1, :], q_rest[:]).then_inc(q_second, 1)
                if b is not None:
                    exps(b, 3)
                    for q in range(2):
                        act.wait_ge(pv_done, 4 * b + 2 * q + 2)
                        copy(oT_raw[:, q, :], o_ps[q][:]).then_inc(o_copied, 1)
                if m is not None:
                    act.wait_ge(mxt_ready, m + 1)
                    act.wait_ge(m_stored, 16 * m)
                    A(m_parts[:, 0, :], work_a[0:32, 0:P], ACT.Copy, scale=-1.0).then_inc(m_first, 1)
                if b is not None:
                    act.wait_ge(turned, 2 * b + 1)
                    copy(oT[:], work_b[:]).then_inc(turn_taken, 1)
                if m is not None:
                    act.wait_ge(m_rest_done, m + 1)
                    copy(m_parts[:, 1, :], m_rest[:]).then_inc(m_second, 1)
                if b is not None:
                    act.wait_ge(turned, 2 * b + 2)
                    copy(fT[:], work_b[0:COMBOS * NF, :]).then_inc(turn_taken, 1)

            turns(act, turn)

        @block.vector
        def _(dve):
            V = nc.vector
            stepped = [0]
            GATE_STEPS = 27

            def step(ins, b):
                stepped[0] += 1
                ins.then_inc(gate_step, 1)
                dve.wait_ge(gate_step, b * GATE_STEPS + stepped[0])

            V.memset(k_ops[96:128, :, :], 1.0).then_inc(ones_done, 1)
            V.memset(feat[:, :, NF - 1:NF], 1.0).then_inc(ones_done, 1)
            V.memset(v_ops[:], 0.0).then_inc(ones_done, 1)
            dve.wait_ge(ones_done, 3)
            V.memset(v_ops[:, :, :, E:E + 1], 1.0).then_inc(ones_done, 1)
            dve.wait_ge(ones_done, 4)
            dve.wait_ge(loaded, 16 * (LOADS - 1))
            V.tensor_copy(gate_parts[:, 0], w_gate[:]).then_inc(gate_split, 1)
            dve.wait_ge(gate_split, 1)
            V.tensor_tensor(gate_rest[:], w_gate[:], gate_parts[:, 0], ALU.subtract).then_inc(gate_split, 1)
            dve.wait_ge(gate_split, 2)
            V.tensor_copy(gate_parts[:, 1], gate_rest[:]).then_inc(gate_split, 1)
            dve.wait_ge(gate_split, 3)
            V.tensor_tensor(gate_parts[:, 2], gate_rest[:], gate_parts[:, 1], ALU.subtract).then_inc(gate_split, 1)
            dve.wait_ge(v_ready, 1)
            for kt in range(2):
                V.tensor_tensor(v_ops[0:KT0, kt, :, 0:E], s_ps[kt][0:KT0, 0:D].rearrange("p (h e) -> p h e", h=HEADS),
                                par[0:KT0, BV0:BV0 + D].rearrange("p (h e) -> p h e", h=HEADS), ALU.add).then_inc(kv_done, 1)
            dve.wait_ge(kv_done, 3)
            V.tensor_copy(k_parts[:, 0, :], kf[:]).then_inc(half_done, 1)
            dve.wait_ge(half_done, 2)
            V.tensor_tensor(k_rest[:], kf[:], k_parts[:, 0, :], ALU.subtract).then_inc(half_done, 1)
            dve.wait_ge(half_done, 3)
            V.tensor_copy(k_parts[:, 1, :], k_rest[:]).then_inc(half_done, 1)
            dve.wait_ge(half_done, 4)
            V.tensor_tensor(k_parts[:, 2, :], k_rest[:], k_parts[:, 1, :], ALU.subtract).then_inc(kparts_done, 1)

            def statistics(x, n):
                for a in range(QT):
                    last = V.bn_stats(stats[:, a, :], x[:, a, :])
                last.then_inc(stats_done, 1)
                dve.wait_ge(stats_done, n)
                dve.nop(nofuse=True)
                for a in range(QT):
                    last = V.bn_aggr(mv[:, a, :], stats[:, a, :])
                last.then_inc(mv_done, 1)

            def normalise(out, x, n):
                dve.wait_ge(rstd_done, n)
                for a in range(QT):
                    last = V.tensor_scalar(out[:, a, :], x[:, a, :], mv[:, a, 0:1], rstd[:, a:a + 1],
                                           ALU.subtract, ALU.mult)
                return last

            def maxima(m, n):
                for tile in range(QT):
                    t = n * QT + tile
                    dve.wait_ge(s_ready, m * 16 + t + 1)
                    V.reduce_max(mx[:].rearrange("p (h a) -> p h a", a=QT)[:, 2 * n:2 * n + 2, tile],
                                 s_ps[t % 2][:, 0:2 * S_KEYS].rearrange("p (i t) -> p i t", i=2), AX.X).then_inc(s_taken, 1)

            def convolve(c):
                dve.wait_ge(gathered, 16 * TAPS * QT * (c + 1))
                dve.wait_ge(hb_done, c)
                V.tensor_tensor(h0[:], taps_in[:, 0], taps_in[:, 1], ALU.add).then_inc(conv_step, 1)
                dve.wait_ge(conv_step, c + 1)
                V.tensor_tensor(h0[:], h0[:], taps_in[:, 2], ALU.add).then_inc(h0_done, 1)
                dve.wait_ge(h0_done, c + 1)

            def turn(a, m, b, pa, roots, more):
                stepped[0] = 0
                if m is not None:
                    for n in range(3):
                        maxima(m, n)
                if a is not None:
                    dve.wait_ge(q_first, a + 1)
                    V.tensor_tensor(q_rest[:], qf[:], q_parts[:, 0, :], ALU.subtract).then_inc(q_rest_done, 1)
                if m is not None:
                    maxima(m, 3)
                if b is not None:
                    for q in range(2):
                        src = work_b[:].rearrange("p (a j w) -> p a j w", a=QT, j=4)
                        dve.wait_ge(oq_ready, 2 * b + q + 1)
                        step(V.reciprocal(rz[:, q, :, :], src[:, :, :, E]), b)
                        V.tensor_tensor(o_tok[:].rearrange("p a (q j e) -> p a q j e", q=2, j=4)[:, :, q], src[:, :, :, 0:E],
                                        rz[:, q, :, :].unsqueeze(3).to_broadcast([P, QT, 4, E]), ALU.mult).then_inc(oq_taken, 1)
                if m is not None:
                    dve.wait_ge(m_first, m + 1)
                    V.scalar_tensor_tensor(out=m_rest[:], in0=work_a[0:32, 0:P], scalar=-1.0, in1=m_parts[:, 0, :],
                                           op0=ALU.mult, op1=ALU.subtract).then_inc(m_rest_done, 1)
                if b is not None:
                    dve.wait_ge(wo_ready, b + 1)
                    dve.wait_ge(hb_done, b + 1)
                    V.tensor_tensor(h1[:], work3[:], hb[pa][:], ALU.add).then_inc(h1_done, 1)
                    dve.wait_ge(h1_done, b + 1)
                    statistics(h1, roots + 1)
                    step(normalise(x_bd, h1, roots + 1), b)
                    roots = roots + 1
                    step(V.scalar_tensor_tensor(out=bits[:], in0=x_bd[:, :, 16:80], scalar=0.5,
                                                in1=par[:, FIRST0:FIRST0 + 64].unsqueeze(1).to_broadcast([P, QT, 64]),
                                                op0=ALU.is_gt, op1=ALU.mult), b)
                    step(V.reduce_max(first[:], bits[:].rearrange("p a (n j) -> p (a n) j", j=16), AX.X), b)
                    step(V.tensor_scalar(left[:], first[:], -1.0, 16.0, ALU.mult, ALU.add), b)
                    step(V.scalar_tensor_tensor(out=feat[:, :, 0:4], in0=first[:].rearrange("p (a n) -> p a n", a=QT),
                                                scalar=0.0, in1=left[:].rearrange("p (a n) -> p a n", a=QT),
                                                op0=ALU.is_gt, op1=ALU.mult), b)
                    step(V.tensor_copy(feat[:, :, 4:7], x_bd[:, :, 1:4]), b)
                    step(V.tensor_copy(feat_parts[:, :, 0], feat[:]), b)
                    step(V.tensor_tensor(feat_rest[:], feat[:], feat_parts[:, :, 0], ALU.subtract), b)
                    step(V.tensor_copy(feat_parts[:, :, 1], feat_rest[:]), b)
                    V.tensor_tensor(feat_ops[:, :, 5], feat_rest[:], feat_parts[:, :, 1], ALU.subtract)
                    V.tensor_copy(feat_ops[:, :, 0:3], feat_parts[:, :, 0].unsqueeze(2).to_broadcast([P, QT, 3, NF]))
                    V.tensor_copy(feat_ops[:, :, 3:5], feat_parts[:, :, 1].unsqueeze(2).to_broadcast([P, QT, 2, NF])).then_inc(feat_done, 1)
                    step(V.tensor_single_scalar(on[:], x_bd[:, :, 1:4], 0.5, ALU.is_gt), b)
                    step(V.tensor_scalar(off[:], on[:], -1.0, 1.0, ALU.mult, ALU.add), b)
                    step(V.tensor_copy(pick[:, :, 0:1], on[:, :, 0:1]), b)
                    step(V.tensor_tensor(pick[:, :, 1:2], on[:, :, 1:2], off[:, :, 0:1], ALU.mult), b)
                    step(V.tensor_tensor(pick[:, :, 2:3], off[:, :, 1:2], off[:, :, 0:1], ALU.mult), b)
                    step(V.reduce_max(any_on[:], on[:], AX.X), b)
                    step(V.tensor_scalar(mark[:], x_bd[:, :, 0], 0.5, 2.0, ALU.is_ge, ALU.mult), b)
                    step(V.tensor_tensor(mark[:], mark[:], any_on[:], ALU.mult), b)
                if b is not None:
                    for t in range(2 * QT):
                        tile, i = t // 2, t % 2
                        dve.wait_ge(hid_ready, b * 2 * QT + t + 1)
                        for o in range(OPS3):
                            last = V.scalar_tensor_tensor(out=gated[:, i, o * GE:(o + 1) * GE], in0=s_ps[i][:, o * GE:(o + 1) * GE],
                                                          scalar=0.0, in1=par[:, W2G0 + o * GE:W2G0 + (o + 1) * GE],
                                                          op0=ALU.max, op1=ALU.mult, accum_out=y[:, tile, i, o:o + 1])
                        last.then_inc(hid_taken, 1)
                if more:
                    convolve(a + 1)
                    statistics(h0, roots + 1)
                    if b is None:
                        normalise(y_tok, h0, roots + 1).then_inc(norm_done, 1)
                if b is not None:
                    dve.wait_ge(hid_taken, (b + 1) * 2 * QT)
                    step(V.tensor_tensor(y[:].rearrange("p a i o -> p (a i) o"), y[:].rearrange("p a i o -> p (a i) o"),
                                         par[:, B2G0:B2G0 + OPS3].unsqueeze(1).to_broadcast([P, 2 * QT, OPS3]), ALU.add), b)
                    step(V.tensor_tensor(ysel[:], y[:], pick[:].unsqueeze(2).to_broadcast([P, QT, 2, OPS3]), ALU.mult), b)
                    step(V.reduce_sum(res[:], ysel[:], AX.X), b)
                    step(V.tensor_scalar(res[:], res[:], 0.0, 15.0, ALU.max, ALU.min), b)
                    step(V.tensor_scalar(res[:], res[:], ROUND, ROUND, ALU.add, ALU.subtract), b)
                    step(V.tensor_tensor(hot[:], par[:, IOTA0:IOTA0 + 32].rearrange("p (i j) -> p i j", i=2).unsqueeze(1)
                                         .to_broadcast([P, QT, 2, 16]), res[:].unsqueeze(3).to_broadcast([P, QT, 2, 16]),
                                         ALU.is_equal), b)
                    step(V.tensor_tensor(hot[:].rearrange("p a i j -> p a (i j)"), hot[:].rearrange("p a i j -> p a (i j)"),
                                         mark[:].unsqueeze(2).to_broadcast([P, QT, 32]), ALU.mult), b)
                    step(V.tensor_tensor(x_bd[:, :, 80:112], x_bd[:, :, 80:112], hot[:].rearrange("p a i j -> p a (i j)"),
                                         ALU.add), b)
                    dve.wait_ge(h_stored, 16 * b)
                    V.tensor_tensor(h2[:], h1[:], x_bd[:], ALU.add).then_inc(h2_done, 1)
                    if more:
                        roots = roots + 1
                        normalise(y_tok, h0, roots).then_inc(norm_done, 1)
                    dve.wait_ge(h2_done, b + 1)
                    statistics(h2, roots + 1)
                    dve.wait_ge(x_stored, 16 * b)
                    normalise(x_out, h2, roots + 1).then_inc(x_done, 1)
                    assert stepped[0] == GATE_STEPS, stepped

            convolve(0)
            statistics(h0, 1)
            normalise(y_tok, h0, 1).then_inc(norm_done, 1)
            turns(dve, turn)

        @block.gpsimd
        def _(pool):
            G = nc.gpsimd
            G.memset(half[:], -0.5).then_inc(half_done, 1)

            def gather(s):
                pool.wait_ge(idx_loaded, 16 * (s + 1))
                pool.nop(nofuse=True)
                pool.wait_ge(h0_done, s)
                pool.nop(nofuse=True)
                for k in range(TAPS):
                    for tile in range(QT):
                        c = k * QT + tile
                        G.indirect_dma_start(taps_in[:, k, tile, :], None, taps[k],
                                             bass.IndirectOffsetOnAxis(ap=idx[:, c:c + 1], axis=0)).then_inc(gathered, 16)

            def root(n):
                pool.wait_ge(mv_done, n)
                pool.nop(nofuse=True)
                G.tensor_scalar(rstd[:], mv[:, :, 1], LN_EPS, None, ALU.add).then_inc(pool_step, 1)
                pool.wait_ge(pool_step, n)
                pool.nop(nofuse=True)
                G.tensor_tensor(rstd[:], rstd[:], half[:], ALU.pow).then_inc(rstd_done, 1)

            def turn(a, m, b, pa, roots, more):
                if a is not None:
                    pool.wait_ge(q_second, a + 1)
                    pool.nop(nofuse=True)
                    G.tensor_tensor(q_parts[:, 2, :], q_rest[:], q_parts[:, 1, :], ALU.subtract).then_inc(q_third, 1)
                if m is not None:
                    pool.wait_ge(m_second, m + 1)
                    pool.nop(nofuse=True)
                    G.tensor_tensor(m_parts[:, 2, :], m_rest[:], m_parts[:, 1, :], ALU.subtract).then_inc(m_third, 1)
                if b is not None:
                    root(roots + 1)
                    roots = roots + 1
                if a is not None:
                    if b is not None:
                        pool.wait_ge(h1_done, b + 1)
                        pool.nop(nofuse=True)
                    G.tensor_tensor(hb[pa][:], h0[:], par[:, BOA0:BOA0 + D].unsqueeze(1).to_broadcast([P, QT, D]),
                                    ALU.add).then_inc(hb_done, 1)
                if more:
                    root(roots + 1)
                    roots = roots + 1
                if b is not None:
                    root(roots + 1)
                if more > 1:
                    gather(a + 2)

            gather(0)
            pool.wait_ge(loaded, 16 * (LOADS - 1))
            pool.nop(nofuse=True)
            root(1)
            gather(1)
            turns(pool, turn)


WL0, BL0, GF0, BF0 = 0, D, 2 * D, 3 * D
LPAR = 4 * D


def quantised_layer(nc, par_d, ident_d, x_hist, h_hist, out):
    with ExitStack() as ctx:
        def sb(name, shape, dt=F32):
            return ctx.enter_context(nc.sbuf_tensor(name, shape, dt))

        def sem(name):
            return ctx.enter_context(nc.semaphore(name))

        ident = sb("f_ident", [P, P])
        par = sb("f_par", [P, LPAR])
        ones = sb("f_ones", [P, P])
        sums = sb("f_sums", [P, 2])
        means = sb("f_means", [P, 2])
        wc = sb("f_wc", [P, D])
        pos = sb("f_pos", [P, D])
        neg = sb("f_neg", [P, D])
        w_eff = sb("w_eff", [P, D])
        xf = [sb(f"f_xf{i}", [P, QT, D]) for i in range(2)]
        hh = [sb(f"f_hh{i}", [P, QT, D]) for i in range(2)]
        h3 = [sb(f"f_h3{i}", [P, QT, D]) for i in range(2)]
        rq = [sb(f"f_rq{i}", [P, QT, D]) for i in range(2)]
        fin = [sb(f"f_fin{i}", [P, QT, D]) for i in range(2)]
        xn = sb("f_xn", [P, QT, D])
        xg = sb("f_xg", [P, QT, D])
        yn = sb("f_yn", [P, QT, D])
        yT = sb("f_yT", [P, TOK])
        yb = sb("f_yb", [P, QT, D])
        stats = sb("f_stats", [P, 2 * QT, 6])
        mv = sb("f_mv", [P, 2 * QT, 2])
        rstd = sb("f_rstd", [P, 2 * QT])
        half = sb("f_half", [P, 2 * QT])
        turn_ps = ctx.enter_context(nc.psum_tensor("f_turn", [P, TOK], F32))
        y_ps = [ctx.enter_context(nc.psum_tensor(f"f_y{i}", [P, TOK], F32)) for i in range(2)]
        names = ("loaded in_loaded ones_done sums_done sums_ready w_step w_done half_done stats_done mv_done "
                 "ve_done rstd_done xn_done gx_done xg_done h3_done yn_done turned yT_done y_ready step_done rounded "
                 "fin_done stored")
        (loaded, in_loaded, ones_done, sums_done, sums_ready, w_step, w_done, half_done, stats_done, mv_done,
         ve_done, rstd_done, xn_done, gx_done, xg_done, h3_done, yn_done, turned, yT_done, y_ready, step_done, rounded,
         fin_done, stored) = [sem("f_" + n) for n in names.split()]
        block = ctx.enter_context(nc.Block())
        ROUND_STEPS = 5

        def turns(eng, turn):
            turn(-2, 0, True, False, False)
            turn(-1, 1, True, True, False)
            turn(0, 0, True, True, True)
            turn(1, 1, True, True, True)
            with eng.Fori(1, SEQS // 2 - 2) as pair:
                for b in range(2):
                    turn(pair * 2 + b, b, True, True, True)
            turn(SEQS - 4, 0, True, True, True)
            turn(SEQS - 3, 1, True, True, True)
            turn(SEQS - 2, 0, False, True, True)
            turn(SEQS - 1, 1, False, False, True)

        @block.sync
        def _(sp):
            sp.dma_start(ident[:], ident_d).then_inc(loaded, 16)
            sp.dma_start(par[:], par_d).then_inc(loaded, 16)

            def load(s, b):
                sp.dma_start(xf[b][:], x_hist[LAYERS * SEQS + s].rearrange("p (a b) -> p a b", a=QT)).then_inc(in_loaded, 16)
                sp.dma_start(hh[b][:], h_hist[s].rearrange("p (a b) -> p a b", a=QT)).then_inc(in_loaded, 16)

            load(0, 0)

            def turn(t, b, new, mid, old):
                last = isinstance(t, int) and t == SEQS - 3
                if new and not last:
                    sp.wait_ge(in_loaded, 32 * (t + 3))
                    sp.nop(nofuse=True)
                    sp.wait_ge(xn_done, count(t + 2))
                    sp.nop(nofuse=True)
                    sp.wait_ge(h3_done, count(t + 2))
                    sp.nop(nofuse=True)
                    load(t + 3, 1 - b)
                if old:
                    sp.wait_ge(fin_done, t + 1)
                    sp.nop(nofuse=True)
                    sp.wait_ge(stored, 16 * t)
                    sp.nop(nofuse=True)
                    sp.dma_start(out[t].rearrange("(a p) d -> p a d", p=P), fin[b][:]).then_inc(stored, 16)

            turns(sp, turn)
            sp.wait_ge(stored, 16 * SEQS)

        @block.tensor
        def _(pe):
            mm, tr = nc.tensor.matmul, nc.tensor.transpose
            pe.wait_ge(ones_done, 1)
            pe.wait_ge(sums_done, 3)
            mm(y_ps[0][:, 0:2], ones[:], sums[:], start=True, stop=True).then_inc(sums_ready, 1)
            pe.wait_ge(w_done, 1)

            def turn(t, b, new, mid, old):
                if mid:
                    pe.wait_ge(yn_done, t + 2)
                    for a in range(QT):
                        last = tr(turn_ps[:, a * P:(a + 1) * P], yn[:, a, :], ident[:])
                    last.then_inc(turned, 1)
                    pe.wait_ge(yT_done, t + 2)
                    pe.wait_ge(step_done, count(ROUND_STEPS * t))
                    for a in range(QT):
                        last = mm(y_ps[1 - b][:, a * P:(a + 1) * P], yT[:, a * P:(a + 1) * P], w_eff[:], start=True, stop=True)
                    last.then_inc(y_ready, 1)

            turns(pe, turn)

        @block.scalar
        def _(act):
            def turn(t, b, new, mid, old):
                if mid:
                    act.wait_ge(turned, t + 2)
                    act.wait_ge(y_ready, count(t + 1))
                    nc.scalar.copy(yT[:], turn_ps[:]).then_inc(yT_done, 1)

            turns(act, turn)

        @block.vector
        def _(dve):
            V = nc.vector
            w = par[:, WL0:WL0 + D]
            dve.wait_ge(loaded, 32)
            n = [0]

            def w_link(ins):
                n[0] += 1
                ins.then_inc(w_step, 1)
                dve.wait_ge(w_step, n[0])

            V.memset(ones[:], 1.0).then_inc(ones_done, 1)
            V.reduce_sum(sums[:, 0:1], w, AX.X).then_inc(sums_done, 1)
            V.scalar_tensor_tensor(out=wc[:], in0=w, scalar=-1.0, in1=w, op0=ALU.mult, op1=ALU.max).then_inc(sums_done, 1)
            dve.wait_ge(sums_done, 2)
            V.reduce_sum(sums[:, 1:2], wc[:], AX.X).then_inc(sums_done, 1)
            dve.wait_ge(sums_ready, 1)
            w_link(V.tensor_scalar(means[:], y_ps[0][:, 0:2], 1.0 / (D * D), None, ALU.mult))
            w_link(V.tensor_scalar(wc[:], w, means[:, 0:1], None, ALU.subtract))
            w_link(V.tensor_single_scalar(pos[:], wc[:], 0.0, ALU.is_gt))
            w_link(V.tensor_single_scalar(neg[:], wc[:], 0.0, ALU.is_lt))
            w_link(V.tensor_tensor(pos[:], pos[:], neg[:], ALU.subtract))
            w_link(V.tensor_tensor(pos[:], pos[:], w, ALU.subtract))
            w_link(V.tensor_tensor(pos[:], pos[:], w, ALU.add))
            V.tensor_scalar(w_eff[:], pos[:], means[:, 1:2], None, ALU.mult).then_inc(w_done, 1)

            def turn(t, b, new, mid, old):
                first, end = (0 if mid else QT), (2 * QT if new else QT)
                if mid:
                    dve.wait_ge(xg_done, t + 2)
                    dve.wait_ge(in_loaded, 32 * (t + 2))
                    dve.wait_ge(fin_done, count(t))
                    V.tensor_tensor(h3[1 - b][:], xg[:], hh[1 - b][:], ALU.add).then_inc(h3_done, 1)
                if new:
                    dve.wait_ge(in_loaded, 32 * (t + 3))
                    for a in range(QT):
                        last = V.bn_stats(stats[:, QT + a, :], xf[b][:, a, :])
                if mid:
                    dve.wait_ge(h3_done, t + 2)
                    for a in range(QT):
                        last = V.bn_stats(stats[:, a, :], h3[1 - b][:, a, :])
                if mid or new:
                    last.then_inc(stats_done, 1)
                    dve.wait_ge(stats_done, t + 3)
                    dve.nop(nofuse=True)
                    for a in range(first, end):
                        last = V.bn_aggr(mv[:, a, :], stats[:, a, :])
                    last.then_inc(mv_done, 1)
                if old:
                    dve.wait_ge(y_ready, t + 1)
                    dve.wait_ge(fin_done, count(t - 1))
                    r = rq[b]
                    steps = (
                        lambda: V.tensor_tensor(yb[:], y_ps[b][:].rearrange("p (a d) -> p a d", a=QT),
                                                par[:, BL0:BL0 + D].unsqueeze(1).to_broadcast([P, QT, D]), ALU.add),
                        lambda: V.tensor_scalar(r[:], yb[:], -1.0, 1.0, ALU.max, ALU.min),
                        lambda: V.tensor_scalar(r[:], r[:], 7.0, ROUND, ALU.mult, ALU.add),
                        lambda: V.tensor_scalar(r[:], r[:], ROUND, 1.0 / 7.0, ALU.subtract, ALU.mult),
                        lambda: V.tensor_tensor(r[:], r[:], yb[:], ALU.subtract),
                    )
                    for k, f in enumerate(steps):
                        f().then_inc(step_done, 1)
                        dve.wait_ge(step_done, ROUND_STEPS * t + k + 1)
                    V.tensor_tensor(r[:], r[:], yb[:], ALU.add).then_inc(rounded, 1)
                if mid or new:
                    dve.wait_ge(rstd_done, t + 3)
                if mid:
                    dve.wait_ge(turned, count(t + 1))
                    for a in range(QT):
                        last = V.tensor_scalar(yn[:, a, :], h3[1 - b][:, a, :], mv[:, a, 0:1], rstd[:, a:a + 1],
                                               ALU.subtract, ALU.mult)
                    last.then_inc(yn_done, 1)
                if new:
                    dve.wait_ge(xg_done, count(t + 2))
                    for a in range(QT):
                        last = V.tensor_scalar(xn[:, a, :], xf[b][:, a, :], mv[:, QT + a, 0:1], rstd[:, QT + a:QT + a + 1],
                                               ALU.subtract, ALU.mult)
                    last.then_inc(xn_done, 1)

            turns(dve, turn)

        @block.gpsimd
        def _(pool):
            G = nc.gpsimd
            G.memset(half[:], -0.5).then_inc(half_done, 1)
            pool.wait_ge(half_done, 1)
            pool.wait_ge(loaded, 32)

            def turn(t, b, new, mid, old):
                first, end = (0 if mid else QT), (2 * QT if new else QT)
                if mid or new:
                    pool.wait_ge(mv_done, t + 3)
                    pool.nop(nofuse=True)
                    G.tensor_scalar(rstd[:, first:end], mv[:, first:end, 1], LN_EPS, None, ALU.add).then_inc(ve_done, 1)
                    pool.wait_ge(ve_done, t + 3)
                    pool.nop(nofuse=True)
                    G.tensor_tensor(rstd[:, first:end], rstd[:, first:end], half[:, first:end], ALU.pow).then_inc(rstd_done, 1)
                if old:
                    pool.wait_ge(rounded, t + 1)
                    pool.nop(nofuse=True)
                    pool.wait_ge(stored, count(16 * (t - 1)))
                    pool.nop(nofuse=True)
                    G.tensor_tensor(fin[b][:], rq[b][:], h3[b][:], ALU.add).then_inc(fin_done, 1)
                if new:
                    pool.wait_ge(xn_done, t + 3)
                    pool.nop(nofuse=True)
                    pool.wait_ge(h3_done, count(t + 2))
                    pool.nop(nofuse=True)
                    G.tensor_tensor(xg[:], xn[:], par[:, GF0:GF0 + D].unsqueeze(1).to_broadcast([P, QT, D]),
                                    ALU.mult).then_inc(gx_done, 1)
                    pool.wait_ge(gx_done, t + 3)
                    pool.nop(nofuse=True)
                    G.tensor_tensor(xg[:], xg[:], par[:, BF0:BF0 + D].unsqueeze(1).to_broadcast([P, QT, D]),
                                    ALU.add).then_inc(xg_done, 1)

            turns(pool, turn)


def build(nc, a, out):
    def scratch(name, shape, dt=F32):
        return nc.dram_tensor(name, shape, dt).ap()

    x_hist = scratch("x_hist", [(LAYERS + 1) * SEQS, P, QT * D])
    h_hist = scratch("h_hist", [SEQS, P, QT * D])
    embed_attend_gate(nc, a["ids"], (a["tap0"], a["tap1"], a["tap2"]), a["src_t"], a["val_t"], a["w_kv"], a["tower_par"],
                      a["w_gate"], a["ident"], x_hist, h_hist, scratch("t_scr_q", [COMBOS, P, TOK], BF16),
                      scratch("t_scr_k", [COMBOS, P, S_KEYS], BF16), scratch("t_scr_m", [PARTS, HEADS * QT, P], BF16))
    blocks(nc, a["w_qk"], a["w_v"], a["w_tail"], a["ident"], x_hist, scratch("scr_q", [2, COMBOS, P, TOK], BF16),
           scratch("scr_k", [2, COMBOS, P, TOK], BF16), scratch("scr_m", [2, QUADS, PARTS, 16, P], BF16))
    quantised_layer(nc, a["last_par"], a["ident"], x_hist, h_hist, out)


def lay_out(i):
    rows = lambda v: np.broadcast_to(v[None, :], (P, v.shape[0]))
    cols = lambda v: v[:, None]
    a = {}
    padded = np.pad(np.asarray(i["x"]), ((0, 0), (1, 1)), constant_values=VOCAB)
    windows = np.stack([padded[:, k:k + TOK] for k in range(TAPS)], 1)
    a["ids"] = windows.reshape(SEQS, TAPS, QT, P).transpose(0, 3, 1, 2).reshape(SEQS, P, TAPS * QT)
    table = np.pad(i["L0_tok_conv_w"], ((0, 0), (0, 1), (0, 0)))
    for k in range(TAPS):
        a[f"tap{k}"] = table[:, :, k].T
    turn = np.arange(D).reshape(HEADS, E).T.reshape(-1)
    a["src_t"] = i["L0_attn_source_embedding"].reshape(S_KEYS, LC, P).transpose(2, 1, 0)
    a["val_t"] = i["L0_attn_value_embedding"].reshape(S_KEYS, LC, P).transpose(2, 1, 0)
    a["w_kv"] = np.stack([i["L0_attn_Wk"][:, turn].reshape(LC, P, D).transpose(1, 0, 2),
                          i["L0_attn_Wv"].reshape(LC, P, D).transpose(1, 0, 2)], 1)
    ops = ("and", "or", "xor")
    w2 = np.concatenate([i[f"L0_ffn_{o}_w2"][:, 64] for o in ops])
    b2 = np.stack([i[f"L0_ffn_{o}_b2"][64] for o in ops])
    f32 = np.float32
    a["tower_par"] = np.concatenate([
        i["L0_attn_Wq"][:, turn], i["L0_attn_Wo"], cols(i["L0_attn_bq"][turn]), cols(i["L0_attn_bk"][turn]),
        rows(i["L0_attn_bv"]), rows(i["L0_attn_bo"]), rows(w2), rows(b2),
        rows(np.tile(np.arange(16, 0, -1, dtype=f32), 4)), rows(np.tile(np.arange(16, dtype=f32), 2))], 1)
    w1 = np.concatenate([i[f"L0_ffn_{o}_w1"] for o in ops], 1)
    b1 = np.concatenate([i[f"L0_ffn_{o}_b1"] for o in ops])
    none = np.zeros_like(b1)
    a["w_gate"] = np.stack([np.stack([w1[0], none, w1[1], none, w1[46], w1[44], w1[45], b1]),
                            np.stack([none, w1[0], none, w1[1], w1[46], w1[44], w1[45], b1])], 1)
    L = {n: i["L1_attn_" + n] for n in "Wq Wk Wv rms_w Wo bo diffw g_ffn b_ffn W1 b1 W2 b2 g_f b_f".split()}
    turn1 = np.arange(D).reshape(GROUPS, F).T.reshape(-1)
    t = lambda w: w.transpose(0, 2, 1)
    a["w_qk"] = np.stack([t(L["Wq"][:, turn1]), t(L["Wk"][:, turn1])], 2)
    a["w_v"] = t(L["Wv"])
    a["w_tail"] = np.concatenate([
        t(L["Wo"]), t(L["W1"]), t(L["W2"]).reshape(LAYERS, HT, P, D).transpose(0, 2, 1, 3).reshape(LAYERS, P, HID),
        L["rms_w"].reshape(LAYERS, D, 1), L["g_ffn"][:, :, None], L["b_ffn"][:, :, None],
        L["b1"].reshape(LAYERS, HT, P).transpose(0, 2, 1), np.broadcast_to(L["diffw"][:, None, None], (LAYERS, P, 1)),
        np.broadcast_to(L["bo"][:, None, :], (LAYERS, P, D)), np.broadcast_to(L["b2"][:, None, :], (LAYERS, P, D))], 2)
    a["last_par"] = np.concatenate([i["L1_ffn_weight"], rows(i["L1_ffn_bias"]), rows(L["g_f"]), rows(L["b_f"])], 1)
    a["ident"] = np.eye(P, dtype=f32)
    return {n: np.ascontiguousarray(v) for n, v in a.items()}


def kernel(**inputs):
    import concourse.bacc as bacc
    from concourse.bass_utils import run_bass_kernel_spmd

    arrays = lay_out({n: np.asarray(v) for n, v in inputs.items()})
    nc = bacc.Bacc("TRN2", target_bir_lowering=False, num_devices=1)
    nc.disable_value_cache = True
    aps = {n: nc.dram_tensor("in_" + n, v.shape, mybir.dt.from_np(v.dtype), kind="ExternalInput").ap() for n, v in arrays.items()}
    out = nc.dram_tensor("out", (SEQS, TOK, D), F32, kind="ExternalOutput").ap()
    build(nc, aps, out)
    result = run_bass_kernel_spmd(nc, [{"in_" + n: v for n, v in arrays.items()}], core_ids=[0])
    return result.results[0]["out"]
```
